# Optimizing a Trainium2 kernel written in Bass

```python
import numpy as np
import jax
import jax.numpy as jnp

def _softmax(x, axis=-1):
    return jax.nn.softmax(x, axis=axis)

def _gelu(x):
    return jax.nn.gelu(x, approximate=True)

def _silu(x):
    return jax.nn.silu(x)

def _sigmoid(x):
    return jax.nn.sigmoid(x)

def _layernorm(x, axis=-1, eps=1e-05):
    m = jnp.mean(x, axis=axis, keepdims=True)
    v = jnp.var(x, axis=axis, keepdims=True)
    return (x - m) / jnp.sqrt(v + eps)

def _scatter_add(tgt, idx, src, axis=0):
    return tgt.at[idx].add(src)

def _segment_sum(src, seg, n):
    return jax.ops.segment_sum(src, seg, n)
kernel_name = 'mk_gnn_preln_d2_gnn_r8_2fd842'

def setup_inputs(seed: int=0):
    np.random.seed(seed)
    _w = jnp.asarray

    def _rec_inputs():
        import jax
        import jax.numpy as jnp
        _gk = jax.random.key(seed)
        x = -0.000202 + 1 * jax.random.normal(jax.random.fold_in(_gk, 1), (6250, 128), jnp.float32)
        src = jax.random.randint(jax.random.fold_in(_gk, 2), (200000,), 0, 6250, jnp.int32)
        dst = jax.random.randint(jax.random.fold_in(_gk, 3), (200000,), 0, 6250, jnp.int32)
        _o = jnp.argsort(dst, stable=True)
        src = src[_o]
        dst = dst[_o]
        edge_attr_128 = -5.16925e-05 + 1.00005 * jax.random.normal(jax.random.fold_in(_gk, 12), (200000, 128), jnp.float32)
        edge_weight = jax.random.uniform(jax.random.fold_in(_gk, 14), (200000,), jnp.float32, 0.0, 1)
        return (x, src, dst, edge_attr_128, edge_weight)
    x, src, dst, edge_attr_128, edge_weight = _rec_inputs()

    def _L0_gnn_setup():
        import jax, jax.numpy as jnp
        import numpy as np
        N = 6250
        E = 200000
        D_IN = 128
        D_OUT = 128
        ALPHA = 0.2
        key = jax.random.key(seed)
        k1, k2, k3, k4, k5, k6 = jax.random.split(key, 6)
        stdv_w = 1.0 / np.sqrt(D_OUT)
        stdv_a = 1.0 / np.sqrt(2 * D_OUT)
        x = jax.random.normal(k1, (N, D_IN), dtype=jnp.float32)
        W = jax.random.uniform(k2, (D_IN, D_OUT), minval=-stdv_w, maxval=stdv_w, dtype=jnp.float32)
        a = jax.random.uniform(k3, (1, 2 * D_OUT), minval=-stdv_a, maxval=stdv_a, dtype=jnp.float32)
        adj_vals = jax.random.uniform(k4, (E,), dtype=jnp.float32)
        edge_index = jnp.stack([jax.random.randint(k5, (E,), 0, N, dtype=jnp.int32), jax.random.randint(k6, (E,), 0, N, dtype=jnp.int32)], axis=0)
        return {'x': x, 'W': W, 'a': a, 'adj_vals': adj_vals, 'edge_index': edge_index}
    _L0_gnn_all = _L0_gnn_setup()
    _L0_gnn_in = {k: v for k, v in _L0_gnn_all.items() if k in ('W', 'a')}
    del _L0_gnn_all

    def _L1_gnn_setup():
        import jax, jax.numpy as jnp
        import numpy as np
        N_NODES = 6250
        N_EDGES = 100000
        D = 128
        L = 3
        BN_EPS = 1e-05

        def _bn(h, gamma, beta):
            m = h.mean(axis=0)
            v = h.var(axis=0)
            return gamma * (h - m) * jax.lax.rsqrt(v + BN_EPS) + beta
        key = jax.random.key(seed)
        ks = jax.random.split(key, 12)
        x = jax.random.normal(ks[0], (N_NODES, D), dtype=jnp.float32)
        edge_index = jax.random.randint(ks[1], (2, N_EDGES), 0, N_NODES, dtype=jnp.int64)
        edge_attr = jax.random.normal(ks[2], (N_EDGES, D), dtype=jnp.float32)
        batch = jnp.zeros((N_NODES,), dtype=jnp.int64)
        s = 1.0 / np.sqrt(D)
        W1 = jax.random.uniform(ks[3], (L, D, D), jnp.float32, -s, s)
        b1 = jax.random.uniform(ks[4], (L, D), jnp.float32, -s, s)
        g_mlp = jnp.ones((L, D), jnp.float32)
        be_mlp = jnp.zeros((L, D), jnp.float32)
        W2 = jax.random.uniform(ks[5], (L, D, D), jnp.float32, -s, s)
        b2 = jax.random.uniform(ks[6], (L, D), jnp.float32, -s, s)
        g_out = jnp.ones((L, D), jnp.float32)
        be_out = jnp.zeros((L, D), jnp.float32)
        return {'x': x, 'edge_index': edge_index, 'edge_attr': edge_attr, 'batch': batch, 'W1': W1, 'b1': b1, 'g_mlp': g_mlp, 'be_mlp': be_mlp, 'W2': W2, 'b2': b2, 'g_out': g_out, 'be_out': be_out}
    _L1_gnn_all = _L1_gnn_setup()
    _L1_gnn_in = {k: v for k, v in _L1_gnn_all.items() if k in ('W1', 'b1', 'g_mlp', 'be_mlp', 'W2', 'b2', 'g_out', 'be_out')}
    del _L1_gnn_all
    return {'x': x, 'src': src, 'dst': dst, 'edge_attr_128': edge_attr_128, 'edge_weight': edge_weight, 'L0_gnn_W': _L0_gnn_in['W'], 'L0_gnn_a': _L0_gnn_in['a'], 'L1_gnn_W1': _L1_gnn_in['W1'], 'L1_gnn_b1': _L1_gnn_in['b1'], 'L1_gnn_g_mlp': _L1_gnn_in['g_mlp'], 'L1_gnn_be_mlp': _L1_gnn_in['be_mlp'], 'L1_gnn_W2': _L1_gnn_in['W2'], 'L1_gnn_b2': _L1_gnn_in['b2'], 'L1_gnn_g_out': _L1_gnn_in['g_out'], 'L1_gnn_be_out': _L1_gnn_in['be_out']}

def reference(x, src, dst, edge_attr_128, edge_weight, L0_gnn_W, L0_gnn_a, L1_gnn_W1, L1_gnn_b1, L1_gnn_g_mlp, L1_gnn_be_mlp, L1_gnn_W2, L1_gnn_b2, L1_gnn_g_out, L1_gnn_be_out):
    import jax
    import jax.numpy as jnp

    def _L0_gnn_ref(x, W, a, adj_vals, edge_index):
        import jax, jax.numpy as jnp
        import numpy as np
        N = 6250
        E = 200000
        D_IN = 128
        D_OUT = 128
        ALPHA = 0.2
        h = x @ W
        src = edge_index[0]
        dst = edge_index[1]
        a_src, a_dst = (a[0, :D_OUT], a[0, D_OUT:])
        score = h[src] @ a_src + h[dst] @ a_dst
        edge_e = jnp.exp(-jax.nn.leaky_relu(score, negative_slope=ALPHA)) * adj_vals
        e_rowsum = jax.ops.segment_sum(edge_e, src, num_segments=N)[:, None]
        h_prime = jax.ops.segment_sum(edge_e[:, None] * h[dst], src, num_segments=N)
        zero_row = e_rowsum == 0.0
        e_rowsum = jnp.where(zero_row, 1.0, e_rowsum)
        h_prime = jnp.where(zero_row, h, h_prime)
        h_prime = h_prime / e_rowsum
        return jax.nn.elu(h_prime)

    def _L1_gnn_ref(x, edge_index, edge_attr, batch, W1, b1, g_mlp, be_mlp, W2, b2, g_out, be_out):
        import jax, jax.numpy as jnp
        import numpy as np
        N_NODES = 6250
        N_EDGES = 100000
        D = 128
        L = 3
        BN_EPS = 1e-05

        def _bn(h, gamma, beta):
            m = h.mean(axis=0)
            v = h.var(axis=0)
            return gamma * (h - m) * jax.lax.rsqrt(v + BN_EPS) + beta
        src, dst = (edge_index[0], edge_index[1])
        for i in range(L):
            msg = jax.nn.relu(x[src] + edge_attr)
            aggr = jax.ops.segment_sum(msg, dst, num_segments=N_NODES)
            h = x + aggr
            h = h @ W1[i] + b1[i]
            h = jax.nn.relu(_bn(h, g_mlp[i], be_mlp[i]))
            h = h @ W2[i] + b2[i]
            h = _bn(h, g_out[i], be_out[i])
            if i != L - 1:
                h = jax.nn.relu(h)
            x = h
        return x
    edge_index = jnp.stack([src, dst])
    batch0 = jnp.zeros((6250,), jnp.int32)
    h = jnp.maximum(_layernorm(x, axis=-1), 0.0)
    x = x + _L0_gnn_ref(h, L0_gnn_W, L0_gnn_a, edge_weight, edge_index)
    h = jnp.maximum(_layernorm(x, axis=-1), 0.0)
    x = x + _L1_gnn_ref(h, edge_index, edge_attr_128, batch0, L1_gnn_W1, L1_gnn_b1, L1_gnn_g_mlp, L1_gnn_be_mlp, L1_gnn_W2, L1_gnn_b2, L1_gnn_g_out, L1_gnn_be_out)
    return x

_drawn_inputs = setup_inputs


def setup_inputs(seed=0):
    import zlib

    import numpy as np

    out = dict(_drawn_inputs(seed))
    spreads = {'L1_gnn_g_mlp': (1.0, 0.2),
     'L1_gnn_be_mlp': (0.0, 0.1),
     'L1_gnn_g_out': (1.0, 0.2),
     'L1_gnn_be_out': (0.0, 0.1)}
    factors = {'L0_gnn_a': 8.0, 'L1_gnn_b1': 8.0, 'L1_gnn_b2': 8.0}
    for name, (base, spread) in spreads.items():
        noise = np.random.default_rng([zlib.crc32(name.encode()), seed]).standard_normal(out[name].shape)
        drawn = base * np.exp(spread * noise) if base else spread * noise
        out[name] = jnp.asarray(drawn.astype(out[name].dtype))
    for name, factor in factors.items():
        out[name] = (out[name] * factor).astype(out[name].dtype)
    return out
```

```python
from contextlib import ExitStack

import concourse.bass as bass
from concourse import mybir

ALU = mybir.AluOpType
ACT = mybir.ActivationFunctionType
AX = mybir.AxisListType
F32 = mybir.dt.float32
I32 = mybir.dt.int32
RED = bass.bass_isa.ReduceOp

P = 128
D = 128
NODES = 6250
EDGES = 200000
LAYERS = 3
BLOCKS = -(-NODES // P)
LAST = NODES - (BLOCKS - 1) * P
COLS = BLOCKS * P
CHUNK = 512
CHUNKS = -(-COLS // CHUNK)
U = 11
GROUP = P * U
GROUPS = EDGES // GROUP
PAIRS = GROUPS // 2
TAIL = EDGES - GROUPS * GROUP
TAIL_AT = GROUPS * GROUP
ROW = 136
ONE, SCORE = D, D + 1
TABLES = 3
ACC_ROWS = 50 * P
ACC_CHUNK = 10
WINDOW = 128
MAX_WINDOWS = -(-NODES // WINDOW)
AGG_COLS = 50 * ROW
LN_EPS = 1e-05
BN_EPS = 1e-05
ALPHA = 0.2

assert GROUPS % 2 == 0 and 0 < TAIL < P and AGG_COLS >= NODES + WINDOW and ACC_ROWS >= NODES + P


def build(nc, x, src, dst, edge_attr, edge_weight, W, a, W1, b1, g_mlp, be_mlp, W2, b2, g_out, be_out, out):
    ctx = ExitStack()
    with ctx:
        def sb(name, shape, dt=F32):
            return ctx.enter_context(nc.sbuf_tensor(name, shape, dt))

        def sem(name):
            return ctx.enter_context(nc.semaphore(name))

        att_rows = nc.dram_tensor("att_rows", (COLS, ROW), F32).ap()
        gin_rows = [nc.dram_tensor(f"gin_rows{n}", (NODES, D), F32).ap() for n in range(LAYERS)]
        tables = [[nc.dram_tensor(f"sums_by_src{s}{j}", (ACC_ROWS, ROW), F32).ap() for j in range(TABLES)]
                  for s in range(2)]

        agg = sb("agg", [P, AGG_COLS])
        nodes = sb("nodes", [P, BLOCKS, D])
        work = sb("work", [P, AGG_COLS])
        att = sb("att", [P, BLOCKS, ROW])
        gath = sb("gath", [P, 2, U, ROW])
        attr = sb("attr", [P, 2, U, D])
        val = sb("val", [P, U, ROW])
        sent = sb("sent", [P, 2, U, ROW])
        srcb = sb("srcb", [P, 2, GROUP], I32)
        lo = sb("lo", [P, GROUP], I32)
        lo_hot = sb("lo_hot", [P, GROUP])
        match = sb("match", [P, U, P])
        masked = sb("masked", [P, U, P])
        hot = masked
        dst_rel = sb("dst_rel", [P, GROUPS + 1, U])
        dst_all = srcb[:, :, :].rearrange("p s e -> p (s e)")[:, 0:(GROUPS + 1) * U].rearrange("p (g k) -> p g k", k=U)
        src_i = sb("src_i", [P, 2, U], I32)
        dst_i = sb("dst_i", [P, 2, U], I32)
        wgt = sb("wgt", [P, 2, U])
        src_f = sb("src_f", [P, U])
        hi = sb("hi", [P, U], I32)
        hi_hot = sb("hi_hot", [P, U, BLOCKS])
        hi_prod = sb("hi_prod", [P, U, BLOCKS])
        rank = sb("rank", [P, U])
        to_own = sb("to_own", [P, U])
        moved = sb("moved", [P, U])
        sum_idx = sb("sum_idx", [P, 2, U], I32)
        s_src = sb("s_src", [P, U])
        z = sb("z", [P, U])
        zl = sb("zl", [P, U])
        ez = sb("ez", [P, U])
        e = sb("e", [P, U])
        s1 = sb("s1", [P, BLOCKS])
        stat = sb("stat", [P, 8, BLOCKS])
        ident = sb("ident", [P, P])
        lower = sb("lower", [P, P])
        iota_row = sb("iota_row", [P, P])
        iota_p = sb("iota_p", [P, 1])
        own_row = sb("own_row", [P, 1])
        shifts = sb("shifts", [P, MAX_WINDOWS + 1])
        dmax = sb("dmax", [P, GROUPS + 1])
        dneg = sb("dneg", [P, GROUPS + 1])
        gmax = sb("gmax", [P, GROUPS + 1])
        gneg = sb("gneg", [P, GROUPS + 1])
        win_f = sb("win_f", [1, 4, GROUPS + 1])
        base_i = sb("base_i", [1, GROUPS + 1], I32)
        span_i = sb("span_i", [1, GROUPS + 1], I32)
        count_i = sb("count_i", [1, GROUPS + 1], I32)
        first_i = sb("first_i", [1, GROUPS + 1], I32)
        W_sb = sb("W_sb", [P, D])
        a_sb = sb("a_sb", [P, 2 * D])
        W1_sb = sb("W1_sb", [P, LAYERS, D])
        W2_sb = sb("W2_sb", [P, LAYERS, D])
        par = sb("par", [P, 6, LAYERS])
        bn = sb("bn", [P, CHUNKS, 6])
        bn_mv = sb("bn_mv", [P, 2])
        bn_t = sb("bn_t", [P, 6])
        ps = ctx.enter_context(nc.psum_tensor("ps", [P, 8, CHUNK], F32))

        ps_score = ps[:, 0:2, :].rearrange("p b (k c) -> p (b k) c", c=64)
        PER = CHUNK // ROW
        flat = work[:, :]

        s_nodes, s_dsts, s_small = sem("nodes_loaded"), sem("dsts_loaded"), sem("weights_loaded")
        s_const, s_pad, s_zero, s_zeroed = sem("constants"), sem("nodes_padded"), sem("zeros_set"), sem("tables_zeroed")
        s_step = sem("vector_step")
        s_att_row, s_gin_row = sem("att_rows_stored"), [sem(f"gin_rows_stored{n}") for n in range(LAYERS)]
        s_extent, s_extents = sem("extents_by_partition"), sem("extents_of_groups")
        s_windows = sem("windows_listed")
        s_var, s_std = sem("variance_ready"), sem("deviation_ready")
        s_normed = [sem(f"normed{n}") for n in range(2)]
        TURNS = ["att_in", "gin_in"] + [f"gin_out{n}" for n in range(LAYERS)]
        s_turned = {t: sem(f"turned_{t}") for t in TURNS}
        s_copied = {t: sem(f"turned_copied_{t}") for t in TURNS}
        s_h, s_h_kept, s_att_ready = sem("h_product"), sem("h_kept"), sem("att_ready")
        s_cols = [sem(f"edge_columns_loaded{s}") for s in range(2)]
        s_srcf, s_hi, s_lo, s_lohot = sem("src_f_ready"), sem("hi_ready"), sem("lo_ready"), sem("lo_hot_ready")
        s_match, s_masked, s_rank = sem("match_ready"), sem("masked_ready"), sem("rank_ready")
        s_own, s_moved, s_idx = sem("to_own_ready"), sem("moved_ready"), sem("sum_idx_ready")
        s_hihot, s_hisel, s_score, s_ssrc = sem("hi_hot_ready"), sem("hi_prod_ready"), sem("scores_by_block"), sem("s_src_ready")
        s_z, s_zl, s_ez, s_e = sem("z_ready"), sem("leaky_ready"), sem("exp_ready"), sem("e_ready")
        s_val = [sem(f"val_ready{s}") for s in range(2)]
        s_sums, s_sent = sem("equal_sources_summed"), [sem(f"sent_ready{s}") for s in range(2)]
        s_gath = [sem(f"att_gathered{s}") for s in range(2)]
        s_added = [[sem(f"added_to_table{s}{j}") for j in range(TABLES)] for s in range(2)]
        s_table, s_tabled = sem("table_loaded"), sem("table_summed")
        s_min, s_expm = sem("elu_min_ready"), sem("elu_exp_ready")
        s_resid = sem("residual_ready")
        s_g = [[sem(f"gathered{n}{s}") for s in range(2)] for n in range(LAYERS)]
        s_idxs = [[sem(f"src_loaded{n}{s}") for s in range(2)] for n in range(LAYERS)]
        s_attr = [[sem(f"attr_loaded{n}{s}") for s in range(2)] for n in range(LAYERS)]
        s_raw = [[sem(f"message_summed{n}{s}") for s in range(2)] for n in range(LAYERS)]
        s_msg = [[sem(f"message_ready{n}{s}") for s in range(2)] for n in range(LAYERS)]
        s_free = [[sem(f"message_used{n}{s}") for s in range(2)] for n in range(LAYERS)]
        s_hot = [sem(f"hot_ready{n}") for n in range(LAYERS)]
        s_win = [sem(f"window_summed{n}") for n in range(LAYERS)]
        s_agg = [sem(f"window_added{n}") for n in range(LAYERS)]
        s_mm = [[sem(f"product{n}{m}") for m in range(2)] for n in range(LAYERS)]
        s_mmk = [[sem(f"product_kept{n}{m}") for m in range(2)] for n in range(LAYERS)]
        s_bnv = [[sem(f"bn_var{n}{m}") for m in range(2)] for n in range(LAYERS)]
        s_bns = [[sem(f"bn_std{n}{m}") for m in range(2)] for n in range(LAYERS)]
        s_bnp = [[sem(f"bn_scale{n}{m}") for m in range(2)] for n in range(LAYERS)]
        s_act = [[sem(f"normed_kept{n}{m}") for m in range(2)] for n in range(LAYERS)]
        s_out = sem("out_stored")
        s_pool = sem("pool_may_go")

        block = ctx.enter_context(nc.Block())

        def column(i, n, u=U):
            return n

        def edges(ap, i, slot):
            at = (2 * i + slot) * GROUP
            return ap[at:at + GROUP] if isinstance(i, int) else ap[bass.ds(at, GROUP)]

        def adds_of(j, u=U):
            return len(range(j, u, TABLES))

        def by_block(t):
            return t.rearrange("p (b d) -> p b d", d=D)

        def width(c):
            return min(CHUNK, NODES - c * CHUNK)

        def blocks_of(c):
            return [(b, LAST if b == BLOCKS - 1 else P) for b in range(4 * c, min(4 * c + 4, BLOCKS))]

        @block.sync
        def _(sp):
            def store_rows(to, done):
                sp.dma_start(to[0:whole].rearrange("(b p) d -> p b d", p=P), by_block(flat[:, 0:whole])).then_inc(done, 16)
                sp.dma_start(to[whole:NODES], flat[0:LAST, whole:whole + D]).then_inc(done, 16)

            sp.wait_ge(s_pad, 1)
            whole = (BLOCKS - 1) * P
            sp.dma_start(nodes[:, 0:BLOCKS - 1, :], x[0:whole].rearrange("(b p) d -> p b d", p=P)).then_inc(s_nodes, 16)
            sp.dma_start(nodes[0:LAST, BLOCKS - 1, :], x[whole:NODES]).then_inc(s_nodes, 16)
            sp.dma_start(W_sb[:, :], W).then_inc(s_small, 16)
            sp.dma_start(a_sb[:, :], a[0].partition_broadcast(P)).then_inc(s_small, 16)
            sp.dma_start(W1_sb[:, :, :], W1.rearrange("l d n -> d l n")).then_inc(s_small, 16)
            sp.dma_start(W2_sb[:, :, :], W2.rearrange("l d n -> d l n")).then_inc(s_small, 16)
            with nc.allow_non_contiguous_dma(reason="six small parameters by feature"):
                for n, t in enumerate((b1, g_mlp, be_mlp, b2, g_out, be_out)):
                    sp.dma_start(par[:, n, :], t.rearrange("l d -> d l")).then_inc(s_small, 16)
            sp.dma_start(dst_all[:, 0:GROUPS, :], dst[0:TAIL_AT].rearrange("(g p k) -> p g k", p=P, k=U)).then_inc(s_dsts, 16)
            sp.dma_start(dst_all[0:TAIL, GROUPS, 0:1], dst[TAIL_AT:EDGES].rearrange("(p k) -> p k", k=1)).then_inc(s_dsts, 16)
            sp.wait_ge(s_zero, 1)
            zeros = attr[:, 0, :, :].rearrange("p k d -> p (k d)")[:, 0:ACC_CHUNK * ROW]
            for t in tables[0] + tables[1]:
                v = t.rearrange("(p q r) c -> q p (r c)", p=P, r=ACC_CHUNK)
                for q in range(ACC_ROWS // P // ACC_CHUNK):
                    sp.dma_start(v[q], zeros).then_inc(s_zeroed, 16)
            sp.wait_ge(s_att_ready, 1)
            sp.dma_start(att_rows.rearrange("(b p) c -> p b c", p=P), att[:, :, :]).then_inc(s_att_row, 16)

            def load_columns(i, slot, p, u, part):
                sp.wait_ge(s_val[slot], i)
                for to, of in ((src_i, src), (dst_i, dst), (wgt, edge_weight)):
                    sp.dma_start(to[0:p, slot, 0:u], part(of).rearrange("(p k) -> p k", k=u)).then_inc(s_cols[slot], 16)
                sp.dma_start(srcb[:, slot, 0:p * u], part(src).partition_broadcast(P)).then_inc(s_cols[slot], 16)

            for slot in range(2):
                load_columns(0, slot, P, U, lambda of: edges(of, 0, slot))
            with sp.Fori(1, PAIRS) as i:
                for slot in range(2):
                    load_columns(i, slot, P, U, lambda of: edges(of, i, slot))
            load_columns(PAIRS, 0, TAIL, 1, lambda of: of[TAIL_AT:EDGES])

            for s in range(2):
                for j in range(TABLES):
                    sp.wait_ge(s_added[s][j], 16 * (adds_of(j) * PAIRS + (1 if s == 0 and j == 0 else 0)))
            for n, t in enumerate(tables[0] + tables[1]):
                if n >= 2:
                    sp.wait_ge(s_tabled, n - 1)
                else:
                    sp.wait_ge(s_h_kept, CHUNKS)
                to = agg if n == 0 else work
                sp.dma_start(to[:, 0:BLOCKS * ROW].rearrange("p (b c) -> p b c", c=ROW),
                             t[0:COLS].rearrange("(b p) c -> p b c", p=P)).then_inc(s_table, 16)
            sp.wait_ge(s_normed[1], 1)
            store_rows(gin_rows[0], s_gin_row[0])

            for n in range(LAYERS):
                def load_group(i, slot, p, u, part, part_attr):
                    sp.wait_ge(s_raw[n][slot], i)
                    sp.dma_start(src_i[0:p, slot, 0:u], part(src).rearrange("(p k) -> p k", k=u)).then_inc(s_idxs[n][slot], 16)
                    sp.dma_start(attr[0:p, slot, 0:u, :], part_attr.rearrange("(p k) d -> p k d", k=u)).then_inc(s_attr[n][slot], 16)

                for slot in range(2):
                    load_group(0, slot, P, U, lambda of: edges(of, 0, slot), edge_attr[slot * GROUP:(slot + 1) * GROUP, :])
                with sp.Fori(1, PAIRS) as i:
                    for slot in range(2):
                        load_group(i, slot, P, U, lambda of: edges(of, i, slot),
                                   edge_attr[bass.ds((2 * i + slot) * GROUP, GROUP), :])
                load_group(PAIRS, 0, TAIL, 1, lambda of: of[TAIL_AT:EDGES], edge_attr[TAIL_AT:EDGES, :])
                sp.wait_ge(s_copied[f"gin_out{n}"], CHUNKS)
                to, done = (gin_rows[n + 1], s_gin_row[n + 1]) if n + 1 < LAYERS else (out, s_out)
                store_rows(to, done)
            for n in range(LAYERS):
                sp.wait_ge(s_gin_row[n], 32)
            sp.wait_ge(s_out, 32)

        @block.gpsimd
        def _(pool):
            pool.memset(ident[:, :], 1.0).then_inc(s_const, 1)
            pool.memset(lower[:, :], 1.0).then_inc(s_const, 1)
            pool.wait_ge(s_const, 2)
            pool.affine_select(out=ident[:, :], in_=ident[:, :], compare_op=ALU.is_equal, fill=0.0,
                               base=0, pattern=[[-1, P]], channel_multiplier=1).then_inc(s_const, 1)
            pool.affine_select(out=lower[:, :], in_=lower[:, :], compare_op=ALU.is_gt, fill=0.0,
                               base=0, pattern=[[-1, P]], channel_multiplier=1).then_inc(s_const, 1)
            pool.iota(iota_row[:, :], [[1, P]], base=0, channel_multiplier=0,
                      allow_small_or_imprecise_dtypes=True).then_inc(s_const, 1)
            pool.iota(iota_p[:, :], [[1, 1]], base=0, channel_multiplier=1,
                      allow_small_or_imprecise_dtypes=True).then_inc(s_const, 1)
            pool.iota(own_row[:, :], [[1, 1]], base=NODES, channel_multiplier=1,
                      allow_small_or_imprecise_dtypes=True).then_inc(s_const, 1)
            pool.iota(shifts[:, :], [[WINDOW, MAX_WINDOWS + 1]], base=0, channel_multiplier=0,
                      allow_small_or_imprecise_dtypes=True).then_inc(s_const, 1)
            pool.wait_ge(s_extent, 1)
            pool.partition_all_reduce(gmax[:, :], dmax[:, :], P, RED.max).then_inc(s_extents, 1)
            pool.partition_all_reduce(gneg[:, :], dneg[:, :], P, RED.max).then_inc(s_extents, 1)

            def gather(i, slot, p, u):
                pool.wait_ge(s_cols[slot], 64 * (i + 1))
                pool.wait_ge(s_val[slot], i)
                pool.wait_ge(s_att_row, 16)
                pool.sem_inc(s_pool, 1)
                for k in range(u):
                    pool.indirect_dma_start(
                        out=gath[0:p, slot, k, :], out_offset=None, in_=att_rows,
                        in_offset=bass.IndirectOffsetOnAxis(ap=dst_i[0:p, slot, k:k + 1], axis=0),
                    ).then_inc(s_gath[slot], 16)

            def add_sums(i, slot, p, u):
                pool.wait_ge(s_sent[slot], 4 * (i + 1))
                pool.wait_ge(s_idx, 2 * i + slot + 1)
                for k in range(u):
                    j = k % TABLES
                    pool.wait_ge(s_added[slot][j], 16 * (adds_of(j) * i + k // TABLES))
                    pool.wait_ge(s_zeroed, 16 * 2 * TABLES * (ACC_ROWS // P // ACC_CHUNK))
                    pool.sem_inc(s_pool, 1)
                    pool.indirect_dma_start(
                        out=tables[slot][j],
                        out_offset=bass.IndirectOffsetOnAxis(ap=sum_idx[0:p, slot, k:k + 1], axis=0),
                        in_=sent[0:p, slot, k, :], in_offset=None, compute_op=ALU.add,
                    ).then_inc(s_added[slot][j], 16)

            def turn_of(i):
                gather(i, 1, P, U)
                add_sums(i, 0, P, U)
                gather(i + 1, 0, P, U)
                add_sums(i, 1, P, U)

            gather(0, 0, P, U)
            turn_of(0)
            with pool.Fori(1, PAIRS - 1) as i:
                turn_of(i)
            gather(PAIRS - 1, 1, P, U)
            add_sums(PAIRS - 1, 0, P, U)
            gather(PAIRS, 0, TAIL, 1)
            add_sums(PAIRS - 1, 1, P, U)
            add_sums(PAIRS, 0, TAIL, 1)

            for n in range(LAYERS):
                def gather_group(i, slot, p, u):
                    pool.wait_ge(s_idxs[n][slot], 16 * (i + 1))
                    pool.wait_ge(s_free[n][slot], i)
                    pool.wait_ge(s_gin_row[n], 32)
                    pool.sem_inc(s_pool, 1)
                    for k in range(u):
                        pool.indirect_dma_start(
                            out=gath[0:p, slot, k, 0:D], out_offset=None, in_=gin_rows[n],
                            in_offset=bass.IndirectOffsetOnAxis(ap=src_i[0:p, slot, k:k + 1], axis=0),
                        ).then_inc(s_g[n][slot], 16)

                for slot in range(2):
                    gather_group(0, slot, P, U)
                with pool.Fori(1, PAIRS) as i:
                    for slot in range(2):
                        gather_group(i, slot, P, U)
                gather_group(PAIRS, 0, TAIL, 1)

        @block.scalar
        def _(act):
            def copy_turned(name, to):
                for c in range(CHUNKS):
                    act.wait_ge(s_turned[name], c + 1)
                    bank = 6 + c % 2
                    n = width(c)
                    act.activation(to[:, c * CHUNK:c * CHUNK + n], ps[:, bank, 0:n], ACT.Copy).then_inc(s_copied[name], 1)

            act.wait_ge(s_var, 1)
            act.activation(stat[:, 4, :], stat[:, 3, :], ACT.Sqrt).then_inc(s_std, 1)
            act.wait_ge(s_normed[0], 1)
            copy_turned("att_in", agg)
            for c in range(CHUNKS):
                act.wait_ge(s_h, c + 1)
                nb = len(blocks_of(c))
                act.activation(att[:, 4 * c:4 * c + nb, 0:D],
                               ps[:, 4 + c % 2, 0:nb * D].rearrange("p (b d) -> p b d", d=D), ACT.Copy).then_inc(s_h_kept, 1)

            def attend(i, slot, p, u):
                act.wait_ge(s_zl, 2 * i + slot + 1)
                act.activation(ez[0:p, 0:u], zl[0:p, 0:u], ACT.Exp, scale=-1.0).then_inc(s_ez, 1)
                act.wait_ge(s_sums, 2 * i + slot + 1)
                for j in range(TABLES):
                    act.wait_ge(s_added[slot][j], 16 * adds_of(j) * i)
                for b in range(4):
                    lo_k, hi_k = PER * b, min(PER * b + PER, U)
                    act.activation(sent[0:p, slot, lo_k:hi_k, :] if u == U else sent[0:p, slot, 0:1, b * 34:b * 34 + 34],
                                   (ps[0:p, 2 + b, 0:(hi_k - lo_k) * ROW] if u == U else ps[0:p, 2, b * 34:b * 34 + 34])
                                   .rearrange("p (k c) -> p k c", c=ROW if u == U else 34), ACT.Copy).then_inc(s_sent[slot], 1)

            for slot in range(2):
                attend(0, slot, P, U)
            with act.Fori(1, PAIRS) as i:
                for slot in range(2):
                    attend(i, slot, P, U)
            attend(PAIRS, 0, TAIL, 1)

            act.wait_ge(s_min, 1)
            act.activation(flat[:, 0:COLS], flat[:, 0:COLS], ACT.Exp).then_inc(s_expm, 1)
            act.wait_ge(s_var, 2)
            act.activation(stat[:, 4, :], stat[:, 3, :], ACT.Sqrt).then_inc(s_std, 1)
            act.wait_ge(s_normed[1], 1)
            copy_turned("gin_in", agg)

            for n in range(LAYERS):
                def messages(i, slot, p, u):
                    act.wait_ge(s_raw[n][slot], i + 1)
                    act.activation(gath[0:p, slot, 0:u, 0:D], gath[0:p, slot, 0:u, 0:D], ACT.Relu).then_inc(s_msg[n][slot], 1)

                with act.Fori(0, PAIRS) as i:
                    for slot in range(2):
                        messages(i, slot, P, U)
                messages(PAIRS, 0, TAIL, 1)

                for m in range(2):
                    to = flat if m == 0 else agg
                    for c in range(CHUNKS):
                        w = width(c)
                        act.wait_ge(s_mm[n][m], c + 1)
                        act.activation(to[:, c * CHUNK:c * CHUNK + w], ps[:, 4 + c % 2, 0:w], ACT.Identity,
                                       bias=par[:, 3 * m, n:n + 1]).then_inc(s_mmk[n][m], 1)
                    act.wait_ge(s_bnv[n][m], 1)
                    act.activation(bn_t[:, 1:2], bn_t[:, 0:1], ACT.Sqrt).then_inc(s_bns[n][m], 1)
                    act.wait_ge(s_bnp[n][m], 1)
                    for c in range(CHUNKS):
                        w = width(c)
                        act.activation(to[:, c * CHUNK:c * CHUNK + w], to[:, c * CHUNK:c * CHUNK + w],
                                       ACT.Identity if m == 1 and n == LAYERS - 1 else ACT.Relu,
                                       bias=bn_t[:, 5:6], scale=bn_t[:, 3:4]).then_inc(s_act[n][m], 1)

        @block.vector
        def _(vec):
            steps = [0]

            def link(ins):
                steps[0] += 1
                ins.then_inc(s_step, 1)
                vec.wait_ge(s_step, steps[0])

            def spread(t, n):
                return t.unsqueeze(2).to_broadcast([P, BLOCKS, n])

            def norm(n):
                h3 = by_block(flat[:, 0:COLS])
                sq = by_block(agg[:, 0:COLS])
                link(vec.tensor_reduce(stat[:, 0, :], nodes[:, :, :], AX.X, ALU.add))
                link(vec.tensor_scalar(stat[:, 1, :], stat[:, 0, :], 1.0 / D, None, ALU.mult))
                link(vec.tensor_tensor(h3, nodes[:, :, :], spread(stat[:, 1, :], D), ALU.subtract))
                link(vec.tensor_tensor(sq, h3, h3, ALU.mult))
                link(vec.tensor_reduce(stat[:, 2, :], sq, AX.X, ALU.add))
                vec.tensor_scalar(stat[:, 3, :], stat[:, 2, :], 1.0 / D, LN_EPS, ALU.mult, ALU.add).then_inc(s_var, 1)
                vec.wait_ge(s_std, n + 1)
                link(vec.reciprocal(stat[:, 5, :], stat[:, 4, :]))
                vec.scalar_tensor_tensor(h3, h3, 0.0, spread(stat[:, 5, :], D), ALU.max, ALU.mult).then_inc(s_normed[n], 1)

            vec.memset(nodes[96:P, BLOCKS - 1, :], 0.0).then_inc(s_pad, 1)
            vec.memset(attr[:, 0, :, :], 0.0).then_inc(s_zero, 1)
            vec.memset(dmax[:, :], 0.0)
            vec.memset(dneg[:, :], -float(NODES))
            vec.memset(att[:, :, ONE:ROW], 0.0)
            link(vec.memset(dst_rel[:, :, :], 0.0))
            link(vec.memset(att[:, :, ONE:ONE + 1], 1.0))
            vec.wait_ge(s_dsts, 32)
            vec.tensor_copy(dst_rel[:, 0:GROUPS, :], dst_all[:, 0:GROUPS, :])
            link(vec.tensor_copy(dst_rel[0:TAIL, GROUPS, 0:1], dst_all[0:TAIL, GROUPS, 0:1]))
            vec.tensor_reduce(dmax[:, 0:GROUPS], dst_rel[:, 0:GROUPS, :], AX.X, ALU.max)
            vec.tensor_copy(dmax[0:TAIL, GROUPS:GROUPS + 1], dst_rel[0:TAIL, GROUPS, 0:1])
            link(vec.tensor_reduce(dneg[:, 0:GROUPS], dst_rel[:, 0:GROUPS, :], AX.X, ALU.min))
            vec.tensor_scalar(dneg[:, 0:GROUPS], dneg[:, 0:GROUPS], -1.0, None, ALU.mult)
            vec.tensor_scalar(dneg[0:TAIL, GROUPS:GROUPS + 1], dst_rel[0:TAIL, GROUPS, 0:1], -1.0, None,
                              ALU.mult).then_inc(s_extent, 1)

            vec.wait_ge(s_nodes, 32)
            norm(0)

            vec.wait_ge(s_extents, 2)
            link(vec.tensor_tensor(dst_rel[:, :, :], dst_rel[:, :, :],
                                   gneg[:, :].unsqueeze(2).to_broadcast([P, GROUPS + 1, U]), ALU.add))
            vec.tensor_scalar(base_i[:, :], gneg[0:1, :], -1.0, None, ALU.mult)
            link(vec.tensor_tensor(span_i[:, :], gmax[0:1, :], gneg[0:1, :], ALU.add))
            link(vec.tensor_scalar(span_i[:, :], span_i[:, :], WINDOW.bit_length() - 1, None, ALU.logical_shift_right))
            link(vec.tensor_scalar(win_f[:, 0, :], span_i[:, :], 1.0, None, ALU.add))
            vec.tensor_copy(count_i[:, :], win_f[:, 0, :])
            link(vec.memset(win_f[:, 1, :], 0.0))
            link(vec.tensor_tensor_scan(win_f[:, 2, :], win_f[:, 0, :], win_f[:, 1, :], 0.0, ALU.add, ALU.add))
            link(vec.tensor_tensor(win_f[:, 3, :], win_f[:, 2, :], win_f[:, 0, :], ALU.subtract))
            vec.tensor_scalar(first_i[:, :], win_f[:, 3, :], 1.0, None, ALU.add).then_inc(s_windows, 1)

            vec.wait_ge(s_small, 160)
            vec.wait_ge(s_h_kept, CHUNKS)
            prod = by_block(flat[:, 0:COLS])
            vec.wait_ge(s_copied["att_in"], CHUNKS)
            h3 = att[:, :, 0:D]
            link(vec.tensor_tensor(prod, h3, a_sb[:, 0:D].unsqueeze(1).to_broadcast([P, BLOCKS, D]), ALU.mult))
            link(vec.tensor_reduce(s1[:, :], prod, AX.X, ALU.add))
            link(vec.tensor_tensor(prod, h3, a_sb[:, D:2 * D].unsqueeze(1).to_broadcast([P, BLOCKS, D]), ALU.mult))
            vec.tensor_reduce(att[:, :, SCORE], prod, AX.X, ALU.add).then_inc(s_att_ready, 1)

            vec.wait_ge(s_const, 8)

            def attend(i, slot, p, u):
                g = 2 * i + slot
                vec.wait_ge(s_cols[slot], 64 * (i + 1))
                src_row = srcb[:, slot, 0:p * u]
                src_kj = src_row.rearrange("p (j k) -> p k j", k=u)
                vec.tensor_copy(src_f[0:p, 0:u], src_i[0:p, slot, 0:u]).then_inc(s_srcf, 1)
                vec.tensor_scalar(hi[0:p, 0:u], src_i[0:p, slot, 0:u], 7, None, ALU.logical_shift_right).then_inc(s_hi, 1)
                vec.tensor_scalar(lo[:, 0:p * u], src_row, P - 1, None, ALU.bitwise_and).then_inc(s_lo, 1)
                vec.wait_ge(s_score, g)
                vec.wait_ge(s_lo, g + 1)
                vec.tensor_scalar(lo_hot[:, 0:p * u], lo[:, 0:p * u], iota_p[:, 0:1], None, ALU.is_equal).then_inc(s_lohot, 1)
                vec.wait_ge(s_sums, g)
                vec.wait_ge(s_srcf, g + 1)
                vec.tensor_tensor(match[0:p, 0:u, 0:p], src_kj[0:p], src_f[0:p, 0:u].unsqueeze(2).to_broadcast([p, u, p]),
                                  ALU.is_equal).then_inc(s_match, 1)
                vec.wait_ge(s_match, g + 1)
                vec.tensor_tensor(masked[0:p, 0:u, 0:p], match[0:p, 0:u, 0:p],
                                  lower[0:p, 0:p].unsqueeze(1).to_broadcast([p, u, p]), ALU.mult).then_inc(s_masked, 1)
                vec.wait_ge(s_masked, g + 1)
                vec.tensor_reduce(rank[0:p, 0:u], masked[0:p, 0:u, 0:p], AX.X, ALU.add).then_inc(s_rank, 1)
                vec.tensor_scalar(to_own[0:p, 0:u], src_f[0:p, 0:u], -1.0, own_row[0:p, 0:1], ALU.mult, ALU.add).then_inc(s_own, 1)
                vec.wait_ge(s_rank, g + 1)
                vec.wait_ge(s_own, g + 1)
                vec.scalar_tensor_tensor(moved[0:p, 0:u], rank[0:p, 0:u], 1.0, to_own[0:p, 0:u], ALU.min, ALU.mult).then_inc(s_moved, 1)
                vec.wait_ge(s_moved, g + 1)
                for j in range(TABLES):
                    vec.wait_ge(s_added[slot][j], 16 * adds_of(j) * i)
                vec.tensor_tensor(sum_idx[0:p, slot, 0:u], moved[0:p, 0:u], src_f[0:p, 0:u], ALU.add).then_inc(s_idx, 1)
                vec.wait_ge(s_hi, g + 1)
                vec.tensor_tensor(hi_hot[0:p, 0:u, :], iota_row[0:p, 0:BLOCKS].unsqueeze(1).to_broadcast([p, u, BLOCKS]),
                                  hi[0:p, 0:u].unsqueeze(2).to_broadcast([p, u, BLOCKS]), ALU.is_equal).then_inc(s_hihot, 1)
                vec.wait_ge(s_hihot, g + 1)
                vec.wait_ge(s_score, g + 1)
                vec.tensor_tensor(hi_prod[0:p, 0:u, :], hi_hot[0:p, 0:u, :], ps_score[0:p, 0:u, 0:BLOCKS], ALU.mult).then_inc(s_hisel, 1)
                vec.wait_ge(s_hisel, g + 1)
                vec.tensor_reduce(s_src[0:p, 0:u], hi_prod[0:p, 0:u, :], AX.X, ALU.add).then_inc(s_ssrc, 1)
                vec.wait_ge(s_ssrc, g + 1)
                vec.wait_ge(s_gath[slot], 16 * (U * i + u))
                vec.tensor_tensor(z[0:p, 0:u], s_src[0:p, 0:u], gath[0:p, slot, 0:u, SCORE], ALU.add).then_inc(s_z, 1)
                vec.wait_ge(s_z, g + 1)
                vec.scalar_tensor_tensor(zl[0:p, 0:u], z[0:p, 0:u], ALPHA, z[0:p, 0:u], ALU.mult, ALU.max).then_inc(s_zl, 1)
                vec.wait_ge(s_ez, g + 1)
                vec.tensor_tensor(e[0:p, 0:u], ez[0:p, 0:u], wgt[0:p, slot, 0:u], ALU.mult).then_inc(s_e, 1)
                vec.wait_ge(s_e, g + 1)
                vec.tensor_tensor(val[0:p, 0:u, :], gath[0:p, slot, 0:u, :],
                                  e[0:p, 0:u].unsqueeze(2).to_broadcast([p, u, ROW]), ALU.mult).then_inc(s_val[slot], 1)

            for slot in range(2):
                attend(0, slot, P, U)
            with vec.Fori(1, PAIRS) as i:
                for slot in range(2):
                    attend(i, slot, P, U)
            attend(PAIRS, 0, TAIL, 1)

            sums = agg[:, 0:BLOCKS * ROW]
            for t in range(1, 2 * TABLES):
                vec.wait_ge(s_table, 16 * (t + 1))
                vec.tensor_tensor(sums, sums, work[:, 0:BLOCKS * ROW], ALU.add).then_inc(s_tabled, 1)
                vec.wait_ge(s_tabled, t)
            s3 = sums.rearrange("p (b c) -> p b c", c=ROW)
            w3 = by_block(flat[:, 0:COLS])
            link(vec.tensor_scalar(stat[:, 0, :], s3[:, :, ONE], 0.0, None, ALU.is_equal))
            vec.tensor_scalar(stat[:, 2, :], stat[:, 0, :], -1.0, 1.0, ALU.mult, ALU.add)
            link(vec.tensor_tensor(stat[:, 1, :], s3[:, :, ONE], stat[:, 0, :], ALU.add))
            link(vec.reciprocal(stat[:, 3, :], stat[:, 1, :]))
            link(vec.tensor_tensor(s3[:, :, 0:D], s3[:, :, 0:D], spread(stat[:, 2, :], D), ALU.mult))
            link(vec.tensor_tensor(w3, att[:, :, 0:D], spread(stat[:, 0, :], D), ALU.mult))
            link(vec.tensor_tensor(s3[:, :, 0:D], s3[:, :, 0:D], w3, ALU.add))
            link(vec.tensor_tensor(s3[:, :, 0:D], s3[:, :, 0:D], spread(stat[:, 3, :], D), ALU.mult))
            vec.tensor_scalar(w3, s3[:, :, 0:D], 0.0, None, ALU.min).then_inc(s_min, 1)
            vec.scalar_tensor_tensor(nodes[:, :, :], s3[:, :, 0:D], 0.0, nodes[:, :, :], ALU.max, ALU.add).then_inc(s_resid, 1)
            vec.wait_ge(s_expm, 1)
            vec.wait_ge(s_resid, 1)
            link(vec.scalar_tensor_tensor(nodes[:, :, :], w3, -1.0, nodes[:, :, :], ALU.add, ALU.add))
            norm(1)

            for n in range(LAYERS):
                vec.wait_ge(s_copied["gin_in"] if n == 0 else s_act[n - 1][1], CHUNKS)
                vec.sem_inc(s_agg[n], 1)

                def group(i, slot, p, u, base, first, count, rel):
                    vec.wait_ge(s_g[n][slot], 16 * (U * i + u))
                    vec.wait_ge(s_attr[n][slot], 16 * (i + 1))
                    vec.tensor_tensor(gath[0:p, slot, 0:u, 0:D], gath[0:p, slot, 0:u, 0:D], attr[0:p, slot, 0:u, :],
                                      ALU.add).then_inc(s_raw[n][slot], 1)
                    with vec.Fori(0, count) as w:
                        vec.scalar_tensor_tensor(
                            hot[0:p, 0:u, :], rel.unsqueeze(2).to_broadcast([p, u, WINDOW]), shifts[0:p, bass.ds(w, 1)],
                            iota_row[0:p, 0:WINDOW].unsqueeze(1).to_broadcast([p, u, WINDOW]),
                            ALU.subtract, ALU.is_equal).then_inc(s_hot[n], 1)
                        vec.wait_ge(s_win[n], first + w)
                        vec.wait_ge(s_agg[n], first + w)
                        part = agg[:, bass.ds(nc.s_assert_within(base + w * WINDOW, 0, NODES - 1, skip_runtime_bounds_check_because="a window begins at a destination or before one"), WINDOW)]
                        vec.tensor_tensor(part, part, ps[:, 0, 0:WINDOW], ALU.add).then_inc(s_agg[n], 1)
                    vec.sem_inc(s_free[n][slot], 1)

                def listed(t, g, most):
                    return vec.value_load(t[0:1, g], min_val=0, max_val=most)

                vec.wait_ge(s_windows, 1)
                with vec.Fori(0, PAIRS) as i:
                    for slot in range(2):
                        at = bass.ds(2 * i + slot, 1)
                        group(i, slot, P, U, listed(base_i, at, NODES - 1), listed(first_i, at, GROUPS * MAX_WINDOWS),
                              listed(count_i, at, MAX_WINDOWS), dst_rel[:, at, :].rearrange("p a k -> p (a k)"))
                at = slice(GROUPS, GROUPS + 1)
                group(PAIRS, 0, TAIL, 1, listed(base_i, at, NODES - 1), listed(first_i, at, GROUPS * MAX_WINDOWS),
                      listed(count_i, at, MAX_WINDOWS), dst_rel[0:TAIL, GROUPS, 0:1])

                for m in range(2):
                    to = flat if m == 0 else agg
                    for c in range(CHUNKS):
                        w = width(c)
                        vec.wait_ge(s_mmk[n][m], c + 1)
                        ins = vec.bn_stats(bn[:, c, :], to[:, c * CHUNK:c * CHUNK + w])
                    link(ins)
                    link(vec.bn_aggr(bn_mv[:, :], bn[:, :, :].rearrange("p c s -> p (c s)")))
                    vec.tensor_scalar(bn_t[:, 0:1], bn_mv[:, 1:2], BN_EPS, None, ALU.add).then_inc(s_bnv[n][m], 1)
                    vec.wait_ge(s_bns[n][m], 1)
                    link(vec.reciprocal(bn_t[:, 2:3], bn_t[:, 1:2]))
                    link(vec.tensor_tensor(bn_t[:, 3:4], bn_t[:, 2:3], par[:, 3 * m + 1, n:n + 1], ALU.mult))
                    link(vec.tensor_tensor(bn_t[:, 4:5], bn_mv[:, 0:1], bn_t[:, 3:4], ALU.mult))
                    vec.tensor_tensor(bn_t[:, 5:6], par[:, 3 * m + 2, n:n + 1], bn_t[:, 4:5], ALU.subtract).then_inc(s_bnp[n][m], 1)

                name = f"gin_out{n}"
                for c in range(CHUNKS):
                    vec.wait_ge(s_turned[name], c + 1)
                    for b, size in blocks_of(c):
                        to = flat[0:size, b * D:(b + 1) * D]
                        of = ps[0:size, 6 + c % 2, (b % 4) * D:(b % 4 + 1) * D]
                        if n == LAYERS - 1:
                            ins = vec.tensor_tensor(to, of, nodes[0:size, b, :], ALU.add)
                        else:
                            ins = vec.tensor_copy(to, of)
                    ins.then_inc(s_copied[name], 1)

        @block.tensor
        def _(pe):
            def turn(name, of):
                for c in range(CHUNKS):
                    if c >= 2:
                        pe.wait_ge(s_copied[name], c - 1)
                    for b, size in blocks_of(c):
                        ins = of(b, size, ps[:, 6 + c % 2, (b % 4) * P:(b % 4 + 1) * P])
                    ins.then_inc(s_turned[name], 1)

            def to_features(b, size, to):
                return pe.transpose(to[:, 0:P], flat[:, b * D:(b + 1) * D], ident[:, :])

            def to_nodes(b, size, to):
                return pe.transpose(to[0:size, :], agg[:, b * P:b * P + size], ident[:, :])

            pe.wait_ge(s_const, 3)
            pe.wait_ge(s_normed[0], 1)
            turn("att_in", to_features)
            pe.wait_ge(s_small, 160)
            for c in range(CHUNKS):
                pe.wait_ge(s_copied["att_in"], c + 1)
                if c >= 2:
                    pe.wait_ge(s_h_kept, c - 1)
                for b, size in blocks_of(c):
                    ins = pe.matmul(ps[:, 4 + c % 2, (b % 4) * D:(b % 4 + 1) * D], agg[:, b * P:(b + 1) * P], W_sb[:, :],
                                    start=True, stop=True)
                ins.then_inc(s_h, 1)

            pe.wait_ge(s_att_ready, 1)
            pe.wait_ge(s_h_kept, CHUNKS)

            def attend(i, slot, p, u):
                g = 2 * i + slot
                pe.wait_ge(s_lohot, g + 1)
                pe.wait_ge(s_hisel, g)
                hot_kj = lo_hot[:, 0:p * u].rearrange("p (j k) -> p k j", k=u)
                for k in range(u):
                    ins = pe.matmul(ps_score[0:p, k, 0:BLOCKS], hot_kj[:, k, :], s1[:, :], start=True, stop=True)
                ins.then_inc(s_score, 1)
                pe.wait_ge(s_val[slot], i + 1)
                pe.wait_ge(s_match, g + 1)
                pe.wait_ge(s_sent[0], 4 * (i + slot))
                pe.wait_ge(s_sent[1], 4 * i)
                for k in range(u):
                    at = (k % PER) * ROW
                    ins = pe.matmul(ps[0:p, 2 + k // PER, at:at + ROW], match[0:p, k, 0:p], val[0:p, k, :], start=True, stop=True)
                ins.then_inc(s_sums, 1)

            for slot in range(2):
                attend(0, slot, P, U)
            with pe.Fori(1, PAIRS) as i:
                for slot in range(2):
                    attend(i, slot, P, U)
            attend(PAIRS, 0, TAIL, 1)

            pe.wait_ge(s_normed[1], 1)
            turn("gin_in", to_features)

            for n in range(LAYERS):
                def group(i, slot, p, u, first, count):
                    with pe.Fori(0, count) as w:
                        pe.wait_ge(s_msg[n][slot], i + 1)
                        pe.wait_ge(s_hot[n], first + w)
                        pe.wait_ge(s_agg[n], first + w)
                        for k in range(u):
                            ins = pe.matmul(ps[:, 0, 0:WINDOW], gath[0:p, slot, k, 0:D], hot[0:p, k, :],
                                            start=(k == 0), stop=(k == u - 1))
                        ins.then_inc(s_win[n], 1)

                def listed(t, g, most):
                    return pe.value_load(t[0:1, g], min_val=0, max_val=most)

                pe.wait_ge(s_windows, 1)
                with pe.Fori(0, PAIRS) as i:
                    for slot in range(2):
                        at = bass.ds(2 * i + slot, 1)
                        group(i, slot, P, U, listed(first_i, at, GROUPS * MAX_WINDOWS), listed(count_i, at, MAX_WINDOWS))
                at = slice(GROUPS, GROUPS + 1)
                group(PAIRS, 0, TAIL, 1, listed(first_i, at, GROUPS * MAX_WINDOWS), listed(count_i, at, MAX_WINDOWS))

                pe.wait_ge(s_free[n][0], PAIRS + 1)
                last = listed(first_i, at, GROUPS * MAX_WINDOWS) + listed(count_i, at, MAX_WINDOWS)
                pe.wait_ge(s_agg[n], last)
                pe.wait_ge(s_gin_row[n], 32)
                for m in range(2):
                    of, w_sb = (agg, W1_sb) if m == 0 else (flat, W2_sb)
                    for c in range(CHUNKS):
                        w = width(c)
                        if m == 1:
                            pe.wait_ge(s_act[n][0], c + 1)
                        if c >= 2:
                            pe.wait_ge(s_mmk[n][m], c - 1)
                        pe.matmul(ps[:, 4 + c % 2, 0:w], w_sb[:, n, :], of[:, c * CHUNK:c * CHUNK + w],
                                  start=True, stop=True).then_inc(s_mm[n][m], 1)
                pe.wait_ge(s_act[n][1], CHUNKS)
                turn(f"gin_out{n}", to_nodes)


_INS = ["x", "src", "dst", "edge_attr_128", "edge_weight", "L0_gnn_W", "L0_gnn_a", "L1_gnn_W1", "L1_gnn_b1",
        "L1_gnn_g_mlp", "L1_gnn_be_mlp", "L1_gnn_W2", "L1_gnn_b2", "L1_gnn_g_out", "L1_gnn_be_out"]


def kernel(**inputs):
    import numpy as _np
    import concourse.bacc as _bacc
    from concourse import mybir as _mybir
    from concourse.bass_utils import run_bass_kernel_spmd as _run

    nc = _bacc.Bacc("TRN2", target_bir_lowering=False, num_devices=1)
    arrays, args = {}, []
    for name in _INS:
        t = _np.ascontiguousarray(inputs[name])
        arrays[f"in_{name}"] = t
        args.append(nc.dram_tensor(f"in_{name}", t.shape, _mybir.dt.from_np(t.dtype), kind="ExternalInput").ap())
    args.append(nc.dram_tensor("out_nodes", (NODES, D), F32, kind="ExternalOutput").ap())
    build(nc, *args)
    r = _run(nc, [arrays], core_ids=[0])
    return r.results[0]["out_nodes"]
```

```python
from contextlib import ExitStack

import concourse.bass as bass
from concourse import mybir

ALU = mybir.AluOpType
ACT = mybir.ActivationFunctionType
AX = mybir.AxisListType
F32 = mybir.dt.float32
I32 = mybir.dt.int32
I16 = mybir.dt.int16
BF16 = mybir.dt.bfloat16
RED = bass.bass_isa.ReduceOp

P = 128
D = 128
NODES = 6250
EDGES = 200000
LAYERS = 3
BLOCKS = -(-NODES // P)
LAST = NODES - (BLOCKS - 1) * P
COLS = BLOCKS * P
CHUNK = 512
CHUNKS = -(-COLS // CHUNK)
U = 11
GROUP = P * U
GROUPS = EDGES // GROUP
PAIRS = GROUPS // 2
TAIL = EDGES - GROUPS * GROUP
TAIL_AT = GROUPS * GROUP
ROW = D + 2
ONE, SCORE = D, D + 1
TABLES = 6
ACC_ROWS = 50 * P
ACC_CHUNK = 10
ATT_ROWS = 50 * P
WINDOW = 128
MAX_WINDOWS = -(-NODES // WINDOW)
LIST = 125
AGG_COLS = 50 * ROW
LN_EPS = 1e-05
BN_EPS = 1e-05
ALPHA = 0.2

assert EDGES % LIST == 0 and ATT_ROWS >= NODES + WINDOW and GROUPS % 2 == 0 and 0 < TAIL < P and AGG_COLS >= NODES + WINDOW and ACC_ROWS >= NODES + P


def build(nc, x, src, dst, edge_attr, edge_weight, W, a, W1, b1, g_mlp, be_mlp, W2, b2, g_out, be_out, out):
    ctx = ExitStack()
    with ctx:
        def sb(name, shape, dt=F32):
            return ctx.enter_context(nc.sbuf_tensor(name, shape, dt))

        def sem(name):
            return ctx.enter_context(nc.semaphore(name))

        att_rows = nc.dram_tensor("att_rows", (ATT_ROWS, ROW), F32).ap()
        gin_rows = [nc.dram_tensor(f"gin_rows{n}", (NODES, D), F32).ap() for n in range(LAYERS)]
        tables = [nc.dram_tensor(f"sums_by_src{j}", (ACC_ROWS, ROW), F32).ap() for j in range(TABLES)]
        src_list = nc.dram_tensor("src_16_bits", (EDGES,), I16).ap()
        dst_list = nc.dram_tensor("dst_16_bits", (EDGES,), I16).ap()

        agg = sb("agg", [P, AGG_COLS])
        nodes = sb("nodes", [P, BLOCKS, D])
        work = sb("work", [P, AGG_COLS])
        att = sb("att", [P, BLOCKS, ROW])
        gath = sb("gath", [P, 2, U, ROW])
        attr = sb("attr", [P, 2, U, D])
        val = gath[:, 0, :, :]
        sent = sb("sent", [P, 2, U, ROW])
        src_row = sb("src_row", [P, 2, GROUP], I16)
        dst_row = sb("dst_row", [P, 2, GROUP], I16)
        lo = sb("lo", [P, GROUP], I16)
        lo_hot = sb("lo_hot", [P, GROUP])
        dst_hot = [sb(f"dst_hot{s}", [P, GROUP]) for s in range(2)]
        hot = dst_hot[0][:, :].rearrange("p (k c) -> p k c", c=WINDOW)
        window = sb("window", [P, 2, ROW])
        match = sb("match", [P, 2, U, P])
        earlier = sb("earlier", [P, U, P], BF16)
        zeros = sb("zeros", [1, P + CHUNK], BF16)
        dst_rel = sb("dst_rel", [P, GROUPS + 1, U])
        src_all = gath[:, :, :, :].rearrange("p s k c -> p (s k c)").bitcast(I32)
        dst_all = sent[:, :, :, :].rearrange("p s k c -> p (s k c)").bitcast(I32)
        dst_cols = agg[:, 0:(GROUPS + 1) * U].bitcast(I32).rearrange("p (g k) -> p g k", k=U)
        src_i = sb("src_i", [P, 2, U], I32)
        wgt = sb("wgt", [P, 2, U])
        src_f = sb("src_f", [P, U])
        hi = sb("hi", [P, U], I32)
        hi_f = sb("hi_f", [P, U])
        picked = sb("picked", [P, U, BLOCKS])
        rank = sb("rank", [P, U])
        to_own = sb("to_own", [P, U])
        moved = sb("moved", [P, U])
        sum_idx = sb("sum_idx", [P, 2, U], I32)
        s_src = sb("s_src", [P, U])
        z = sb("z", [P, U])
        zl = sb("zl", [P, U])
        ez = sb("ez", [P, U])
        e = sb("e", [P, U])
        s1 = sb("s1", [P, BLOCKS])
        stat = sb("stat", [P, 8, BLOCKS])
        ident = sb("ident", [P, P])
        lower = sb("lower", [P, P])
        iota_row = sb("iota_row", [P, P])
        iota_p = sb("iota_p", [P, 1])
        own_row = sb("own_row", [P, 1])
        shifts = sb("shifts", [P, MAX_WINDOWS + 1])
        dmax = sb("dmax", [P, GROUPS + 1])
        dneg = sb("dneg", [P, GROUPS + 1])
        gmax = sb("gmax", [P, GROUPS + 1])
        gneg = sb("gneg", [P, GROUPS + 1])
        win_f = sb("win_f", [1, 4, GROUPS + 1])
        win_slot = sb("win_slot", [1, 4, GROUPS + 1])
        base_p = sb("base_p", [P, GROUPS + 1])
        slot_first_i = sb("slot_first_i", [1, GROUPS + 1], I32)
        base_i = sb("base_i", [1, GROUPS + 1], I32)
        span_i = sb("span_i", [1, GROUPS + 1], I32)
        count_i = sb("count_i", [1, GROUPS + 1], I32)
        first_i = sb("first_i", [1, GROUPS + 1], I32)
        W_sb = sb("W_sb", [P, D])
        a_sb = sb("a_sb", [P, 2 * D])
        W1_sb = sb("W1_sb", [P, LAYERS, D])
        W2_sb = sb("W2_sb", [P, LAYERS, D])
        par = sb("par", [P, 6, LAYERS])
        bn = sb("bn", [P, CHUNKS, 6])
        bn_mv = sb("bn_mv", [P, 2])
        bn_t = sb("bn_t", [P, 6])
        ps = ctx.enter_context(nc.psum_tensor("ps", [P, 8, CHUNK], F32))

        PER = CHUNK // ROW
        BANKS = -(-U // PER)
        LEFT = (CHUNK - PER * ROW) // BLOCKS

        def given(p, k):
            return ps[0:p, k // PER, k % PER * ROW:(k % PER + 1) * ROW]

        def summed(p, k):
            return ps[0:p, BANKS + k // PER, k % PER * ROW:(k % PER + 1) * ROW]

        def score_bank(k):
            return min(k // LEFT, BANKS - 1)

        def scores(p, k):
            bank = score_bank(k)
            at = (U - (BANKS - 1) * PER if bank == BANKS - 1 else PER) * ROW + (k - bank * LEFT) * BLOCKS
            return ps[0:p, bank, at:at + BLOCKS]

        def spans(u):
            full = u // PER
            return ([(0, full, PER)] if full else []) + ([(full, 1, u % PER)] if u % PER else [])

        flat = work[:, :]

        s_nodes, s_dsts, s_small = sem("nodes_loaded"), sem("dsts_loaded"), sem("weights_loaded")
        s_const, s_pad, s_zero, s_zeroed = sem("constants"), sem("nodes_padded"), sem("zeros_set"), sem("tables_zeroed")
        s_step = sem("vector_step")
        s_att_row, s_gin_row = sem("att_rows_stored"), [sem(f"gin_rows_stored{n}") for n in range(LAYERS)]
        s_extent, s_extents = sem("extents_by_partition"), sem("extents_of_groups")
        s_windows = sem("windows_listed")
        s_var, s_std = sem("variance_ready"), sem("deviation_ready")
        s_normed = [sem(f"normed{n}") for n in range(2)]
        TURNS = ["att_in", "gin_in"] + [f"gin_out{n}" for n in range(LAYERS)]
        s_turned = {t: sem(f"turned_{t}") for t in TURNS}
        s_copied = {t: sem(f"turned_copied_{t}") for t in TURNS}
        s_h, s_h_kept, s_att_ready = sem("h_product"), sem("h_kept"), sem("att_ready")
        s_cols = [sem(f"edge_columns_loaded{s}") for s in range(2)]
        s_lists, s_narrow, s_listed = sem("lists_loaded"), sem("lists_in_16_bits"), sem("lists_stored")
        s_window = [sem(f"window_loaded{s}") for s in range(2)]
        s_dsthot = [sem(f"dst_hot_ready{s}") for s in range(2)]
        s_given = [sem(f"window_given{s}") for s in range(2)]
        s_srcf, s_hi, s_lo, s_lohot = sem("src_f_ready"), sem("hi_ready"), sem("lo_ready"), sem("lo_hot_ready")
        s_match, s_rank = sem("match_ready"), sem("rank_ready")
        s_own, s_moved, s_idx = sem("to_own_ready"), sem("moved_ready"), sem("sum_idx_ready")
        s_hif, s_score, s_ssrc = sem("hi_f_ready"), sem("scores_by_block"), sem("s_src_ready")
        s_z, s_zl, s_ez, s_e = sem("z_ready"), sem("leaky_ready"), sem("exp_ready"), sem("e_ready")
        s_val = [sem(f"val_ready{s}") for s in range(2)]
        s_sums, s_sent = sem("equal_sources_summed"), [sem(f"sent_ready{s}") for s in range(2)]
        s_added = [sem(f"added_to_table{j}") for j in range(TABLES)]
        s_table, s_tabled = sem("table_loaded"), sem("table_summed")
        s_min, s_expm = sem("elu_min_ready"), sem("elu_exp_ready")
        s_resid = sem("residual_ready")
        s_g = [[sem(f"gathered{n}{s}") for s in range(2)] for n in range(LAYERS)]
        s_idxs = [[sem(f"src_loaded{n}{s}") for s in range(2)] for n in range(LAYERS)]
        s_attr = [[sem(f"attr_loaded{n}{s}") for s in range(2)] for n in range(LAYERS)]
        s_raw = [[sem(f"message_summed{n}{s}") for s in range(2)] for n in range(LAYERS)]
        s_msg = [[sem(f"message_ready{n}{s}") for s in range(2)] for n in range(LAYERS)]
        s_free = [[sem(f"message_used{n}{s}") for s in range(2)] for n in range(LAYERS)]
        s_hot = [sem(f"hot_ready{n}") for n in range(LAYERS)]
        s_win = [sem(f"window_summed{n}") for n in range(LAYERS)]
        s_agg = [sem(f"window_added{n}") for n in range(LAYERS)]
        s_mm = sem("product")
        s_mmk = sem("product_kept")
        s_bnv = sem("bn_var")
        s_bns = sem("bn_std")
        s_bnp = sem("bn_scale")
        s_act = sem("normed_kept")
        s_out = sem("out_stored")
        s_pool = sem("pool_may_go")

        block = ctx.enter_context(nc.Block())

        def edges(ap, i, slot):
            at = (2 * i + slot) * GROUP
            return ap[at:at + GROUP] if isinstance(i, int) else ap[bass.ds(at, GROUP)]

        def adds(i, slot, k, j):
            return 16 * (len(range(j, 2 * U, TABLES)) * i + len(range(j, U * slot + k, TABLES)))

        def narrow(t):
            return t[0:LIST, :, :].rearrange("p s e -> p (s e)")[:, 0:EDGES // LIST]

        def window_at(base, w):
            return nc.s_assert_within(base + w * WINDOW, 0, NODES - 1, skip_runtime_bounds_check_because="a window begins at a destination or before one")

        def by_block(t):
            return t.rearrange("p (b d) -> p b d", d=D)

        def chunks_before(n, m):
            return (2 * n + m) * CHUNKS

        def width(c):
            return min(CHUNK, NODES - c * CHUNK)

        def blocks_of(c):
            return [(b, LAST if b == BLOCKS - 1 else P) for b in range(4 * c, min(4 * c + 4, BLOCKS))]

        @block.sync
        def _(sp):
            def store_rows(to, done):
                sp.dma_start(to[0:whole].rearrange("(b p) d -> p b d", p=P), by_block(flat[:, 0:whole])).then_inc(done, 16)
                sp.dma_start(to[whole:NODES], flat[0:LAST, whole:whole + D]).then_inc(done, 16)

            sp.wait_ge(s_pad, 1)
            whole = (BLOCKS - 1) * P
            sp.dma_start(nodes[:, 0:BLOCKS - 1, :], x[0:whole].rearrange("(b p) d -> p b d", p=P)).then_inc(s_nodes, 16)
            sp.dma_start(nodes[0:LAST, BLOCKS - 1, :], x[whole:NODES]).then_inc(s_nodes, 16)
            sp.dma_start(W_sb[:, :], W).then_inc(s_small, 16)
            sp.dma_start(a_sb[:, :], a[0].partition_broadcast(P)).then_inc(s_small, 16)
            sp.dma_start(W1_sb[:, :, :], W1.rearrange("l d n -> d l n")).then_inc(s_small, 16)
            sp.dma_start(W2_sb[:, :, :], W2.rearrange("l d n -> d l n")).then_inc(s_small, 16)
            with nc.allow_non_contiguous_dma(reason="six small parameters by feature"):
                for n, t in enumerate((b1, g_mlp, be_mlp, b2, g_out, be_out)):
                    sp.dma_start(par[:, n, :], t.rearrange("l d -> d l")).then_inc(s_small, 16)
            sp.dma_start(src_all[0:LIST, 0:EDGES // LIST], src.rearrange("(p n) -> p n", p=LIST)).then_inc(s_lists, 16)
            sp.dma_start(dst_all[0:LIST, 0:EDGES // LIST], dst.rearrange("(p n) -> p n", p=LIST)).then_inc(s_lists, 16)
            sp.dma_start(dst_cols[:, 0:GROUPS, :], dst[0:TAIL_AT].rearrange("(g p k) -> p g k", p=P, k=U)).then_inc(s_dsts, 16)
            sp.dma_start(dst_cols[0:TAIL, GROUPS, 0:1], dst[TAIL_AT:EDGES].rearrange("(p k) -> p k", k=1)).then_inc(s_dsts, 16)
            sp.wait_ge(s_zero, 1)
            none = attr[:, 0, :, :].rearrange("p k d -> p (k d)")[:, 0:ACC_CHUNK * ROW]
            for t in tables:
                v = t.rearrange("(p q r) c -> q p (r c)", p=P, r=ACC_CHUNK)
                for q in range(ACC_ROWS // P // ACC_CHUNK):
                    sp.dma_start(v[q], none).then_inc(s_zeroed, 16)
            sp.wait_ge(s_narrow, 2)
            sp.dma_start(src_list.rearrange("(p n) -> p n", p=LIST), narrow(src_row)).then_inc(s_listed, 16)
            sp.dma_start(dst_list.rearrange("(p n) -> p n", p=LIST), narrow(dst_row)).then_inc(s_listed, 16)
            sp.wait_ge(s_att_ready, 1)
            sp.dma_start(att_rows[0:COLS].rearrange("(b p) c -> p b c", p=P), att[:, :, :]).then_inc(s_att_row, 16)
            sp.dma_start(att_rows[COLS:ATT_ROWS], none[:, 0:ROW]).then_inc(s_att_row, 16)
            sp.wait_ge(s_listed, 32)
            sp.wait_ge(s_att_row, 32)
            sp.wait_ge(s_windows, 1)

            def listed(t, g, most):
                return sp.value_load(t[0:1, g], min_val=0, max_val=most)

            def load_columns(i, slot, p, u, part, g):
                sp.wait_ge(s_val[slot], i)
                for to, of in ((src_i, src), (wgt, edge_weight)):
                    sp.dma_start(to[0:p, slot, 0:u], part(of).rearrange("(p k) -> p k", k=u)).then_inc(s_cols[slot], 16)
                for to, of in ((src_row, src_list), (dst_row, dst_list)):
                    sp.dma_start(to[:, slot, 0:p * u], part(of).partition_broadcast(P)).then_inc(s_cols[slot], 16)
                base, first, count = (listed(base_i, g, NODES - 1), listed(slot_first_i, g, GROUPS * MAX_WINDOWS),
                                      listed(count_i, g, MAX_WINDOWS))
                with sp.Fori(0, count) as w:
                    sp.wait_ge(s_given[slot], first + w)
                    sp.dma_start(window[:, slot, :], att_rows[bass.ds(window_at(base, w), WINDOW), :]).then_inc(s_window[slot], 16)

            for slot in range(2):
                load_columns(0, slot, P, U, lambda of: edges(of, 0, slot), slice(slot, slot + 1))
            with sp.Fori(1, PAIRS) as i:
                for slot in range(2):
                    load_columns(i, slot, P, U, lambda of: edges(of, i, slot), bass.ds(2 * i + slot, 1))
            load_columns(PAIRS, 0, TAIL, 1, lambda of: of[TAIL_AT:EDGES], slice(GROUPS, GROUPS + 1))

            for j in range(TABLES):
                sp.wait_ge(s_added[j], adds(PAIRS, 0, 1, j))
            for n, t in enumerate(tables):
                if n >= 2:
                    sp.wait_ge(s_tabled, n - 1)
                else:
                    sp.wait_ge(s_h_kept, CHUNKS)
                to = agg if n == 0 else work
                sp.dma_start(to[:, 0:BLOCKS * ROW].rearrange("p (b c) -> p b c", c=ROW),
                             t[0:COLS].rearrange("(b p) c -> p b c", p=P)).then_inc(s_table, 16)
            sp.wait_ge(s_normed[1], 1)
            store_rows(gin_rows[0], s_gin_row[0])

            for n in range(LAYERS):
                def load_group(i, slot, p, u, part, part_attr):
                    sp.wait_ge(s_raw[n][slot], i)
                    sp.dma_start(src_i[0:p, slot, 0:u], part(src).rearrange("(p k) -> p k", k=u)).then_inc(s_idxs[n][slot], 16)
                    sp.dma_start(attr[0:p, slot, 0:u, :], part_attr.rearrange("(p k) d -> p k d", k=u)).then_inc(s_attr[n][slot], 16)

                for slot in range(2):
                    load_group(0, slot, P, U, lambda of: edges(of, 0, slot), edge_attr[slot * GROUP:(slot + 1) * GROUP, :])
                with sp.Fori(1, PAIRS) as i:
                    for slot in range(2):
                        load_group(i, slot, P, U, lambda of: edges(of, i, slot),
                                   edge_attr[bass.ds((2 * i + slot) * GROUP, GROUP), :])
                load_group(PAIRS, 0, TAIL, 1, lambda of: of[TAIL_AT:EDGES], edge_attr[TAIL_AT:EDGES, :])
                sp.wait_ge(s_copied[f"gin_out{n}"], CHUNKS)
                to, done = (gin_rows[n + 1], s_gin_row[n + 1]) if n + 1 < LAYERS else (out, s_out)
                store_rows(to, done)
            for n in range(LAYERS):
                sp.wait_ge(s_gin_row[n], 32)
            sp.wait_ge(s_out, 32)

        @block.gpsimd
        def _(pool):
            pool.memset(ident[:, :], 1.0).then_inc(s_const, 1)
            pool.memset(lower[:, :], 1.0).then_inc(s_const, 1)
            pool.wait_ge(s_const, 2)
            pool.affine_select(out=ident[:, :], in_=ident[:, :], compare_op=ALU.is_equal, fill=0.0,
                               base=0, pattern=[[-1, P]], channel_multiplier=1).then_inc(s_const, 1)
            pool.affine_select(out=lower[:, :], in_=lower[:, :], compare_op=ALU.is_gt, fill=0.0,
                               base=0, pattern=[[-1, P]], channel_multiplier=1).then_inc(s_const, 1)
            pool.iota(iota_row[:, :], [[1, P]], base=0, channel_multiplier=0,
                      allow_small_or_imprecise_dtypes=True).then_inc(s_const, 1)
            pool.iota(iota_p[:, :], [[1, 1]], base=0, channel_multiplier=1,
                      allow_small_or_imprecise_dtypes=True).then_inc(s_const, 1)
            pool.iota(own_row[:, :], [[1, 1]], base=NODES, channel_multiplier=1,
                      allow_small_or_imprecise_dtypes=True).then_inc(s_const, 1)
            pool.iota(shifts[:, :], [[WINDOW, MAX_WINDOWS + 1]], base=0, channel_multiplier=0,
                      allow_small_or_imprecise_dtypes=True).then_inc(s_const, 1)
            pool.wait_ge(s_extent, 1)
            pool.partition_all_reduce(gmax[:, :], dmax[:, :], P, RED.max).then_inc(s_extents, 1)
            pool.partition_all_reduce(gneg[:, :], dneg[:, :], P, RED.max).then_inc(s_extents, 1)

            def add_sums(i, slot, p, u):
                pool.wait_ge(s_sent[slot], BANKS * (i + 1))
                pool.wait_ge(s_idx, 2 * i + slot + 1)
                pool.wait_ge(s_zeroed, 16 * TABLES * (ACC_ROWS // P // ACC_CHUNK))
                for k in range(u):
                    j = (U * slot + k) % TABLES
                    pool.wait_ge(s_added[j], adds(i, slot, k, j))
                    pool.sem_inc(s_pool, 1)
                    pool.indirect_dma_start(
                        out=tables[j],
                        out_offset=bass.IndirectOffsetOnAxis(ap=sum_idx[0:p, slot, k:k + 1], axis=0),
                        in_=sent[0:p, slot, k, :], in_offset=None, compute_op=ALU.add,
                    ).then_inc(s_added[j], 16)

            for slot in range(2):
                add_sums(0, slot, P, U)
            with pool.Fori(1, PAIRS) as i:
                for slot in range(2):
                    add_sums(i, slot, P, U)
            add_sums(PAIRS, 0, TAIL, 1)

            for n in range(LAYERS):
                def gather_group(i, slot, p, u):
                    pool.wait_ge(s_idxs[n][slot], 16 * (i + 1))
                    pool.wait_ge(s_free[n][slot], i)
                    pool.wait_ge(s_gin_row[n], 32)
                    pool.sem_inc(s_pool, 1)
                    for k in range(u):
                        pool.indirect_dma_start(
                            out=gath[0:p, slot, k, 0:D], out_offset=None, in_=gin_rows[n],
                            in_offset=bass.IndirectOffsetOnAxis(ap=src_i[0:p, slot, k:k + 1], axis=0),
                        ).then_inc(s_g[n][slot], 16)

                for slot in range(2):
                    gather_group(0, slot, P, U)
                with pool.Fori(1, PAIRS) as i:
                    for slot in range(2):
                        gather_group(i, slot, P, U)
                gather_group(PAIRS, 0, TAIL, 1)

        @block.scalar
        def _(act):
            def copy_turned(name, to):
                for c in range(CHUNKS):
                    act.wait_ge(s_turned[name], c + 1)
                    bank = 6 + c % 2
                    n = width(c)
                    act.activation(to[:, c * CHUNK:c * CHUNK + n], ps[:, bank, 0:n], ACT.Copy).then_inc(s_copied[name], 1)

            act.wait_ge(s_var, 1)
            act.activation(stat[:, 4, :], stat[:, 3, :], ACT.Sqrt).then_inc(s_std, 1)
            act.wait_ge(s_normed[0], 1)
            copy_turned("att_in", agg)
            for c in range(CHUNKS):
                act.wait_ge(s_h, c + 1)
                nb = len(blocks_of(c))
                act.activation(att[:, 4 * c:4 * c + nb, 0:D],
                               ps[:, 4 + c % 2, 0:nb * D].rearrange("p (b d) -> p b d", d=D), ACT.Copy).then_inc(s_h_kept, 1)

            def attend(i, slot, p, u):
                act.wait_ge(s_zl, 2 * i + slot + 1)
                act.activation(ez[0:p, 0:u], zl[0:p, 0:u], ACT.Exp, scale=-1.0).then_inc(s_ez, 1)
                act.wait_ge(s_sums, 2 * i + slot + 1)
                if not (isinstance(i, int) and i == 0):
                    for j in range(TABLES):
                        act.wait_ge(s_added[j], adds(i - 1, slot, U, j))
                if u == U:
                    for b in range(BANKS):
                        k, n = PER * b, min(PER, U - PER * b)
                        act.activation(sent[0:p, slot, k:k + n, :], ps[0:p, BANKS + b, 0:n * ROW].rearrange("p (k c) -> p k c", c=ROW),
                                       ACT.Copy).then_inc(s_sent[slot], 1)
                else:
                    act.activation(sent[0:p, slot, 0, :], summed(p, 0), ACT.Copy).then_inc(s_sent[slot], BANKS)

            for slot in range(2):
                attend(0, slot, P, U)
            with act.Fori(1, PAIRS) as i:
                for slot in range(2):
                    attend(i, slot, P, U)
            attend(PAIRS, 0, TAIL, 1)

            act.wait_ge(s_min, 1)
            act.activation(flat[:, 0:COLS], flat[:, 0:COLS], ACT.Exp).then_inc(s_expm, 1)
            act.wait_ge(s_var, 2)
            act.activation(stat[:, 4, :], stat[:, 3, :], ACT.Sqrt).then_inc(s_std, 1)
            act.wait_ge(s_normed[1], 1)
            copy_turned("gin_in", agg)

            for n in range(LAYERS):
                def messages(i, slot, p, u):
                    act.wait_ge(s_raw[n][slot], i + 1)
                    act.activation(gath[0:p, slot, 0:u, 0:D], gath[0:p, slot, 0:u, 0:D], ACT.Relu).then_inc(s_msg[n][slot], 1)

                with act.Fori(0, PAIRS) as i:
                    for slot in range(2):
                        messages(i, slot, P, U)
                messages(PAIRS, 0, TAIL, 1)

                for m in range(2):
                    to = flat if m == 0 else agg
                    for c in range(CHUNKS):
                        w = width(c)
                        act.wait_ge(s_mm, chunks_before(n, m) + c + 1)
                        act.activation(to[:, c * CHUNK:c * CHUNK + w], ps[:, 4 + c % 2, 0:w], ACT.Identity,
                                       bias=par[:, 3 * m, n:n + 1]).then_inc(s_mmk, 1)
                    act.wait_ge(s_bnv, 2 * n + m + 1)
                    act.activation(bn_t[:, 1:2], bn_t[:, 0:1], ACT.Sqrt).then_inc(s_bns, 1)
                    act.wait_ge(s_bnp, 2 * n + m + 1)
                    for c in range(CHUNKS):
                        w = width(c)
                        act.activation(to[:, c * CHUNK:c * CHUNK + w], to[:, c * CHUNK:c * CHUNK + w],
                                       ACT.Identity if m == 1 and n == LAYERS - 1 else ACT.Relu,
                                       bias=bn_t[:, 5:6], scale=bn_t[:, 3:4]).then_inc(s_act, 1)

        @block.vector
        def _(vec):
            steps = [0]

            def link(ins):
                steps[0] += 1
                ins.then_inc(s_step, 1)
                vec.wait_ge(s_step, steps[0])

            def spread(t, n):
                return t.unsqueeze(2).to_broadcast([P, BLOCKS, n])

            def norm(n):
                h3 = by_block(flat[:, 0:COLS])
                sq = by_block(agg[:, 0:COLS])
                link(vec.tensor_reduce(stat[:, 0, :], nodes[:, :, :], AX.X, ALU.add))
                link(vec.tensor_scalar(stat[:, 1, :], stat[:, 0, :], 1.0 / D, None, ALU.mult))
                link(vec.tensor_tensor(h3, nodes[:, :, :], spread(stat[:, 1, :], D), ALU.subtract))
                link(vec.tensor_tensor(sq, h3, h3, ALU.mult))
                link(vec.tensor_reduce(stat[:, 2, :], sq, AX.X, ALU.add))
                vec.tensor_scalar(stat[:, 3, :], stat[:, 2, :], 1.0 / D, LN_EPS, ALU.mult, ALU.add).then_inc(s_var, 1)
                vec.wait_ge(s_std, n + 1)
                link(vec.reciprocal(stat[:, 5, :], stat[:, 4, :]))
                vec.scalar_tensor_tensor(h3, h3, 0.0, spread(stat[:, 5, :], D), ALU.max, ALU.mult).then_inc(s_normed[n], 1)

            vec.memset(nodes[96:P, BLOCKS - 1, :], 0.0).then_inc(s_pad, 1)
            vec.memset(attr[:, 0, :, :], 0.0).then_inc(s_zero, 1)
            vec.memset(dmax[:, :], 0.0)
            vec.memset(dneg[:, :], -float(NODES))
            vec.memset(att[:, :, ONE:ROW], 0.0)
            vec.memset(zeros[:, :], 0.0)
            vec.memset(agg[:, NODES:AGG_COLS], 0.0)
            link(vec.memset(dst_rel[:, :, :], 0.0))
            link(vec.memset(att[:, :, ONE:ONE + 1], 1.0))
            vec.wait_ge(s_dsts, 32)
            vec.tensor_copy(dst_rel[:, 0:GROUPS, :], dst_cols[:, 0:GROUPS, :])
            link(vec.tensor_copy(dst_rel[0:TAIL, GROUPS, 0:1], dst_cols[0:TAIL, GROUPS, 0:1]))
            vec.tensor_reduce(dmax[:, 0:GROUPS], dst_rel[:, 0:GROUPS, :], AX.X, ALU.max)
            vec.tensor_copy(dmax[0:TAIL, GROUPS:GROUPS + 1], dst_rel[0:TAIL, GROUPS, 0:1])
            link(vec.tensor_reduce(dneg[:, 0:GROUPS], dst_rel[:, 0:GROUPS, :], AX.X, ALU.min))
            vec.tensor_scalar(dneg[:, 0:GROUPS], dneg[:, 0:GROUPS], -1.0, None, ALU.mult)
            vec.tensor_scalar(dneg[0:TAIL, GROUPS:GROUPS + 1], dst_rel[0:TAIL, GROUPS, 0:1], -1.0, None,
                              ALU.mult).then_inc(s_extent, 1)

            vec.wait_ge(s_lists, 32)
            for to, of in ((src_row, src_all), (dst_row, dst_all)):
                vec.tensor_copy(narrow(to), of[0:LIST, 0:EDGES // LIST]).then_inc(s_narrow, 1)

            vec.wait_ge(s_nodes, 32)
            norm(0)

            vec.wait_ge(s_extents, 2)
            link(vec.tensor_tensor(dst_rel[:, :, :], dst_rel[:, :, :],
                                   gneg[:, :].unsqueeze(2).to_broadcast([P, GROUPS + 1, U]), ALU.add))
            vec.tensor_scalar(base_i[:, :], gneg[0:1, :], -1.0, None, ALU.mult)
            vec.wait_ge(s_const, 8)
            vec.tensor_scalar(base_p[:, :], gneg[:, :], -1.0, iota_p[:, 0:1], ALU.mult, ALU.add)
            link(vec.tensor_tensor(span_i[:, :], gmax[0:1, :], gneg[0:1, :], ALU.add))
            link(vec.tensor_scalar(span_i[:, :], span_i[:, :], WINDOW.bit_length() - 1, None, ALU.logical_shift_right))
            link(vec.tensor_scalar(win_f[:, 0, :], span_i[:, :], 1.0, None, ALU.add))
            vec.tensor_copy(count_i[:, :], win_f[:, 0, :])
            link(vec.memset(win_f[:, 1, :], 0.0))
            link(vec.tensor_tensor_scan(win_f[:, 2, :], win_f[:, 0, :], win_f[:, 1, :], 0.0, ALU.add, ALU.add))
            link(vec.tensor_tensor(win_f[:, 3, :], win_f[:, 2, :], win_f[:, 0, :], ALU.subtract))
            vec.tensor_scalar(first_i[:, :], win_f[:, 3, :], 1.0, None, ALU.add)
            for slot in range(2):
                of_slot = slice(slot, GROUPS + 1, 2)
                counts = win_f[:, 0, of_slot]
                link(vec.tensor_tensor_scan(win_slot[:, 0, of_slot], counts, win_f[:, 1, of_slot], 0.0, ALU.add, ALU.add))
                link(vec.tensor_tensor(win_slot[:, 1, of_slot], win_slot[:, 0, of_slot], counts, ALU.subtract))
            vec.tensor_scalar(slot_first_i[:, :], win_slot[:, 1, :], 1.0, None, ALU.add).then_inc(s_windows, 1)

            vec.wait_ge(s_small, 160)
            vec.wait_ge(s_h_kept, CHUNKS)
            prod = by_block(flat[:, 0:COLS])
            vec.wait_ge(s_copied["att_in"], CHUNKS)
            h3 = att[:, :, 0:D]
            link(vec.tensor_tensor(prod, h3, a_sb[:, 0:D].unsqueeze(1).to_broadcast([P, BLOCKS, D]), ALU.mult))
            link(vec.tensor_reduce(s1[:, :], prod, AX.X, ALU.add))
            link(vec.tensor_tensor(prod, h3, a_sb[:, D:2 * D].unsqueeze(1).to_broadcast([P, BLOCKS, D]), ALU.mult))
            vec.tensor_reduce(att[:, :, SCORE], prod, AX.X, ALU.add).then_inc(s_att_ready, 1)

            vec.wait_ge(s_windows, 1)

            def listed(t, g, most):
                return vec.value_load(t[0:1, g], min_val=0, max_val=most)

            def attend(i, slot, p, u, at):
                g = 2 * i + slot
                first, count = listed(slot_first_i, at, GROUPS * MAX_WINDOWS), listed(count_i, at, MAX_WINDOWS)
                with vec.Fori(0, count) as w:
                    vec.wait_ge(s_cols[slot], 64 * (i + 1))
                    vec.wait_ge(s_given[slot], first + w)
                    vec.tensor_scalar(dst_hot[slot][:, 0:p * u], dst_row[:, slot, 0:p * u], shifts[:, bass.ds(w, 1)],
                                      base_p[:, at], ALU.subtract, ALU.is_equal).then_inc(s_dsthot[slot], 1)
                src_kj = src_row[0:p, slot, 0:p * u].rearrange("p (j k) -> p k j", k=u)
                vec.tensor_scalar(lo[:, 0:p * u], src_row[:, slot, 0:p * u], P - 1, None, ALU.bitwise_and).then_inc(s_lo, 1)
                vec.tensor_copy(src_f[0:p, 0:u], src_i[0:p, slot, 0:u]).then_inc(s_srcf, 1)
                vec.tensor_scalar(hi[0:p, 0:u], src_i[0:p, slot, 0:u], 7, None, ALU.logical_shift_right).then_inc(s_hi, 1)
                vec.wait_ge(s_score, g)
                vec.wait_ge(s_lo, g + 1)
                vec.tensor_scalar(lo_hot[:, 0:p * u], lo[:, 0:p * u], iota_p[:, 0:1], None, ALU.is_equal).then_inc(s_lohot, 1)
                vec.wait_ge(s_hi, g + 1)
                vec.tensor_copy(hi_f[0:p, 0:u], hi[0:p, 0:u]).then_inc(s_hif, 1)
                if not (isinstance(i, int) and i == 0):
                    vec.wait_ge(s_sums, g - 1)
                vec.wait_ge(s_srcf, g + 1)
                vec.tensor_tensor(match[0:p, slot, 0:u, 0:p], src_kj, src_f[0:p, 0:u].unsqueeze(2).to_broadcast([p, u, p]),
                                  ALU.is_equal).then_inc(s_match, 1)
                for k in range(u):
                    ins = vec.scalar_tensor_tensor(earlier[0:p, k, 0:p], src_kj[:, k, :], src_f[0:p, k:k + 1], lower[0:p, 0:p],
                                                   ALU.is_equal, ALU.mult, accum_out=rank[0:p, k:k + 1])
                ins.then_inc(s_rank, 1)
                vec.tensor_scalar(to_own[0:p, 0:u], src_f[0:p, 0:u], -1.0, own_row[0:p, 0:1], ALU.mult, ALU.add).then_inc(s_own, 1)
                vec.wait_ge(s_hif, g + 1)
                vec.wait_ge(s_score, g + 1)
                vec.wait_ge(s_given[slot], first + count)
                for k in range(u):
                    ins = vec.scalar_tensor_tensor(picked[0:p, k, :], iota_row[0:p, 0:BLOCKS], hi_f[0:p, k:k + 1], scores(p, k),
                                                   ALU.is_equal, ALU.mult, accum_out=s_src[0:p, k:k + 1])
                ins.then_inc(s_ssrc, 1)
                vec.wait_ge(s_rank, g + 1)
                vec.wait_ge(s_own, g + 1)
                vec.scalar_tensor_tensor(moved[0:p, 0:u], rank[0:p, 0:u], 1.0, to_own[0:p, 0:u], ALU.min, ALU.mult).then_inc(s_moved, 1)

                def tiles(t, b, banks, n, bank=0):
                    return t[0:p, b * PER:b * PER + banks * n].rearrange("p (b k) -> p b k", k=n)

                def given_tiles(b, banks, n):
                    return ps[0:p, b:b + banks, 0:n * ROW].rearrange("p b (k c) -> p b k c", c=ROW)

                vec.wait_ge(s_ssrc, g + 1)
                for span in spans(u):
                    ins = vec.tensor_tensor(tiles(z, *span), tiles(s_src, *span), given_tiles(*span)[:, :, :, SCORE], ALU.add)
                ins.then_inc(s_z, 1)
                vec.wait_ge(s_z, g + 1)
                vec.scalar_tensor_tensor(zl[0:p, 0:u], z[0:p, 0:u], ALPHA, z[0:p, 0:u], ALU.mult, ALU.max).then_inc(s_zl, 1)
                vec.wait_ge(s_moved, g + 1)
                if not (isinstance(i, int) and i == 0):
                    for j in range(TABLES):
                        vec.wait_ge(s_added[j], adds(i - 1, slot, U, j))
                vec.tensor_tensor(sum_idx[0:p, slot, 0:u], moved[0:p, 0:u], src_f[0:p, 0:u], ALU.add).then_inc(s_idx, 1)
                vec.wait_ge(s_ez, g + 1)
                vec.tensor_tensor(e[0:p, 0:u], ez[0:p, 0:u], wgt[0:p, slot, 0:u], ALU.mult).then_inc(s_e, 1)
                vec.wait_ge(s_sums, g)
                vec.wait_ge(s_e, g + 1)
                for span in spans(u):
                    b, banks, n = span
                    to = val[0:p, b * PER:b * PER + banks * n, :].rearrange("p (b k) c -> p b k c", k=n)
                    ins = vec.tensor_tensor(to, given_tiles(*span), tiles(e, *span).unsqueeze(3).to_broadcast([p, banks, n, ROW]), ALU.mult)
                ins.then_inc(s_val[slot], 1)

            for slot in range(2):
                attend(0, slot, P, U, slice(slot, slot + 1))
            with vec.Fori(1, PAIRS) as i:
                for slot in range(2):
                    attend(i, slot, P, U, bass.ds(2 * i + slot, 1))
            attend(PAIRS, 0, TAIL, 1, slice(GROUPS, GROUPS + 1))

            sums = agg[:, 0:BLOCKS * ROW]
            for t in range(1, TABLES):
                vec.wait_ge(s_table, 16 * (t + 1))
                vec.tensor_tensor(sums, sums, work[:, 0:BLOCKS * ROW], ALU.add).then_inc(s_tabled, 1)
                vec.wait_ge(s_tabled, t)
            s3 = sums.rearrange("p (b c) -> p b c", c=ROW)
            w3 = by_block(flat[:, 0:COLS])
            link(vec.tensor_scalar(stat[:, 0, :], s3[:, :, ONE], 0.0, None, ALU.is_equal))
            vec.tensor_scalar(stat[:, 2, :], stat[:, 0, :], -1.0, 1.0, ALU.mult, ALU.add)
            link(vec.tensor_tensor(stat[:, 1, :], s3[:, :, ONE], stat[:, 0, :], ALU.add))
            link(vec.reciprocal(stat[:, 3, :], stat[:, 1, :]))
            link(vec.tensor_tensor(s3[:, :, 0:D], s3[:, :, 0:D], spread(stat[:, 2, :], D), ALU.mult))
            link(vec.tensor_tensor(w3, att[:, :, 0:D], spread(stat[:, 0, :], D), ALU.mult))
            link(vec.tensor_tensor(s3[:, :, 0:D], s3[:, :, 0:D], w3, ALU.add))
            link(vec.tensor_tensor(s3[:, :, 0:D], s3[:, :, 0:D], spread(stat[:, 3, :], D), ALU.mult))
            vec.tensor_scalar(w3, s3[:, :, 0:D], 0.0, None, ALU.min).then_inc(s_min, 1)
            vec.scalar_tensor_tensor(nodes[:, :, :], s3[:, :, 0:D], 0.0, nodes[:, :, :], ALU.max, ALU.add).then_inc(s_resid, 1)
            vec.wait_ge(s_expm, 1)
            vec.wait_ge(s_resid, 1)
            link(vec.scalar_tensor_tensor(nodes[:, :, :], w3, -1.0, nodes[:, :, :], ALU.add, ALU.add))
            norm(1)

            for n in range(LAYERS):
                if n == 0:
                    vec.wait_ge(s_copied["gin_in"], CHUNKS)
                else:
                    vec.wait_ge(s_act, chunks_before(n, 0))
                vec.sem_inc(s_agg[n], 1)

                def group(i, slot, p, u, base, first, count, rel):
                    vec.wait_ge(s_g[n][slot], 16 * (U * i + u))
                    vec.wait_ge(s_attr[n][slot], 16 * (i + 1))
                    vec.tensor_tensor(gath[0:p, slot, 0:u, 0:D], gath[0:p, slot, 0:u, 0:D], attr[0:p, slot, 0:u, :],
                                      ALU.add).then_inc(s_raw[n][slot], 1)
                    with vec.Fori(0, count) as w:
                        vec.scalar_tensor_tensor(
                            hot[0:p, 0:u, :], rel.unsqueeze(2).to_broadcast([p, u, WINDOW]), shifts[0:p, bass.ds(w, 1)],
                            iota_row[0:p, 0:WINDOW].unsqueeze(1).to_broadcast([p, u, WINDOW]),
                            ALU.subtract, ALU.is_equal).then_inc(s_hot[n], 1)
                        vec.wait_ge(s_win[n], first + w)
                        vec.wait_ge(s_agg[n], first + w)
                        part = agg[:, bass.ds(window_at(base, w), WINDOW)]
                        vec.tensor_tensor(part, part, ps[:, 0, 0:WINDOW], ALU.add).then_inc(s_agg[n], 1)
                    vec.sem_inc(s_free[n][slot], 1)

                with vec.Fori(0, PAIRS) as i:
                    for slot in range(2):
                        at = bass.ds(2 * i + slot, 1)
                        group(i, slot, P, U, listed(base_i, at, NODES - 1), listed(first_i, at, GROUPS * MAX_WINDOWS),
                              listed(count_i, at, MAX_WINDOWS), dst_rel[:, at, :].rearrange("p a k -> p (a k)"))
                at = slice(GROUPS, GROUPS + 1)
                group(PAIRS, 0, TAIL, 1, listed(base_i, at, NODES - 1), listed(first_i, at, GROUPS * MAX_WINDOWS),
                      listed(count_i, at, MAX_WINDOWS), dst_rel[0:TAIL, GROUPS, 0:1])

                for m in range(2):
                    to = flat if m == 0 else agg
                    for c in range(CHUNKS):
                        w = width(c)
                        vec.wait_ge(s_mmk, chunks_before(n, m) + c + 1)
                        ins = vec.bn_stats(bn[:, c, :], to[:, c * CHUNK:c * CHUNK + w])
                    link(ins)
                    link(vec.bn_aggr(bn_mv[:, :], bn[:, :, :].rearrange("p c s -> p (c s)")))
                    vec.tensor_scalar(bn_t[:, 0:1], bn_mv[:, 1:2], BN_EPS, None, ALU.add).then_inc(s_bnv, 1)
                    vec.wait_ge(s_bns, 2 * n + m + 1)
                    link(vec.reciprocal(bn_t[:, 2:3], bn_t[:, 1:2]))
                    link(vec.tensor_tensor(bn_t[:, 3:4], bn_t[:, 2:3], par[:, 3 * m + 1, n:n + 1], ALU.mult))
                    link(vec.tensor_tensor(bn_t[:, 4:5], bn_mv[:, 0:1], bn_t[:, 3:4], ALU.mult))
                    vec.tensor_tensor(bn_t[:, 5:6], par[:, 3 * m + 2, n:n + 1], bn_t[:, 4:5], ALU.subtract).then_inc(s_bnp, 1)

                name = f"gin_out{n}"
                for c in range(CHUNKS):
                    vec.wait_ge(s_turned[name], c + 1)
                    for b, size in blocks_of(c):
                        to = flat[0:size, b * D:(b + 1) * D]
                        of = ps[0:size, 6 + c % 2, (b % 4) * D:(b % 4 + 1) * D]
                        if n == LAYERS - 1:
                            ins = vec.tensor_tensor(to, of, nodes[0:size, b, :], ALU.add)
                        else:
                            ins = vec.tensor_copy(to, of)
                    ins.then_inc(s_copied[name], 1)

        @block.tensor
        def _(pe):
            def turn(name, of):
                for c in range(CHUNKS):
                    if c >= 2:
                        pe.wait_ge(s_copied[name], c - 1)
                    for b, size in blocks_of(c):
                        ins = of(b, size, ps[:, 6 + c % 2, (b % 4) * P:(b % 4 + 1) * P])
                    ins.then_inc(s_turned[name], 1)

            def to_features(b, size, to):
                return pe.transpose(to[:, 0:P], flat[:, b * D:(b + 1) * D], ident[:, :])

            def to_nodes(b, size, to):
                return pe.transpose(to[0:size, :], agg[:, b * P:b * P + size], ident[:, :])

            pe.wait_ge(s_const, 3)
            pe.wait_ge(s_normed[0], 1)
            turn("att_in", to_features)
            pe.wait_ge(s_small, 160)
            for c in range(CHUNKS):
                pe.wait_ge(s_copied["att_in"], c + 1)
                if c >= 2:
                    pe.wait_ge(s_h_kept, c - 1)
                for b, size in blocks_of(c):
                    ins = pe.matmul(ps[:, 4 + c % 2, (b % 4) * D:(b % 4 + 1) * D], agg[:, b * P:(b + 1) * P], W_sb[:, :],
                                    start=True, stop=True)
                ins.then_inc(s_h, 1)

            pe.wait_ge(s_att_ready, 1)
            pe.wait_ge(s_h_kept, CHUNKS)

            pe.wait_ge(s_windows, 1)

            def listed(t, g, most):
                return pe.value_load(t[0:1, g], min_val=0, max_val=most)

            for slot in range(2):
                pe.sem_inc(s_given[slot], 1)

            def give(i, slot, p, u, at):
                g = 2 * i + slot
                first, count = listed(slot_first_i, at, GROUPS * MAX_WINDOWS), listed(count_i, at, MAX_WINDOWS)
                pe.wait_ge(s_val[1 - slot], i + slot)
                for bank in range(-(-u // PER)):
                    pe.matmul(ps[0:p, bank, :], zeros[:, 0:p], zeros[:, P:P + CHUNK], start=True, stop=False)
                dst_kj = dst_hot[slot][:, 0:p * u].rearrange("p (j k) -> p k j", k=u)
                with pe.Fori(0, count) as w:
                    pe.wait_ge(s_dsthot[slot], first + w)
                    pe.wait_ge(s_window[slot], 16 * (first + w))
                    for k in range(u):
                        ins = pe.matmul(given(p, k), dst_kj[:, k, :], window[:, slot, :], start=False, stop=False)
                    ins.then_inc(s_given[slot], 1)
                pe.wait_ge(s_lohot, g + 1)
                hot_kj = lo_hot[:, 0:p * u].rearrange("p (j k) -> p k j", k=u)
                for k in range(u):
                    ins = pe.matmul(scores(p, k), hot_kj[:, k, :], s1[:, :], start=False,
                                    stop=(k == u - 1 or score_bank(k + 1) != score_bank(k)))
                ins.then_inc(s_score, 1)

            def sum_equal(i, slot, p, u):
                pe.wait_ge(s_val[slot], i + 1)
                pe.wait_ge(s_match, 2 * i + slot + 1)
                pe.wait_ge(s_sent[0], BANKS * (i + slot))
                pe.wait_ge(s_sent[1], BANKS * i)
                for k in range(u):
                    ins = pe.matmul(summed(p, k), match[0:p, slot, k, 0:p], val[0:p, k, :], start=True, stop=True)
                ins.then_inc(s_sums, 1)

            def turn_of(i, at):
                give(i, 1, P, U, at(1))
                sum_equal(i, 0, P, U)
                give(i + 1, 0, P, U, at(2))
                sum_equal(i, 1, P, U)

            give(0, 0, P, U, slice(0, 1))
            turn_of(0, lambda n: slice(n, n + 1))
            with pe.Fori(1, PAIRS - 1) as i:
                turn_of(i, lambda n: bass.ds(2 * i + n, 1))
            give(PAIRS - 1, 1, P, U, slice(GROUPS - 1, GROUPS))
            sum_equal(PAIRS - 1, 0, P, U)
            give(PAIRS, 0, TAIL, 1, slice(GROUPS, GROUPS + 1))
            sum_equal(PAIRS - 1, 1, P, U)
            sum_equal(PAIRS, 0, TAIL, 1)

            pe.wait_ge(s_normed[1], 1)
            turn("gin_in", to_features)

            for n in range(LAYERS):
                def group(i, slot, p, u, first, count):
                    with pe.Fori(0, count) as w:
                        pe.wait_ge(s_msg[n][slot], i + 1)
                        pe.wait_ge(s_hot[n], first + w)
                        pe.wait_ge(s_agg[n], first + w)
                        for k in range(u):
                            ins = pe.matmul(ps[:, 0, 0:WINDOW], gath[0:p, slot, k, 0:D], hot[0:p, k, :],
                                            start=(k == 0), stop=(k == u - 1))
                        ins.then_inc(s_win[n], 1)

                with pe.Fori(0, PAIRS) as i:
                    for slot in range(2):
                        at = bass.ds(2 * i + slot, 1)
                        group(i, slot, P, U, listed(first_i, at, GROUPS * MAX_WINDOWS), listed(count_i, at, MAX_WINDOWS))
                at = slice(GROUPS, GROUPS + 1)
                group(PAIRS, 0, TAIL, 1, listed(first_i, at, GROUPS * MAX_WINDOWS), listed(count_i, at, MAX_WINDOWS))

                pe.wait_ge(s_free[n][0], PAIRS + 1)
                last = listed(first_i, at, GROUPS * MAX_WINDOWS) + listed(count_i, at, MAX_WINDOWS)
                pe.wait_ge(s_agg[n], last)
                pe.wait_ge(s_gin_row[n], 32)
                for m in range(2):
                    of, w_sb = (agg, W1_sb) if m == 0 else (flat, W2_sb)
                    for c in range(CHUNKS):
                        w = width(c)
                        if m == 1:
                            pe.wait_ge(s_act, chunks_before(n, 0) + c + 1)
                        if c >= 2:
                            pe.wait_ge(s_mmk, chunks_before(n, m) + c - 1)
                        pe.matmul(ps[:, 4 + c % 2, 0:w], w_sb[:, n, :], of[:, c * CHUNK:c * CHUNK + w],
                                  start=True, stop=True).then_inc(s_mm, 1)
                pe.wait_ge(s_act, chunks_before(n, 1) + CHUNKS)
                turn(f"gin_out{n}", to_nodes)


_INS = ["x", "src", "dst", "edge_attr_128", "edge_weight", "L0_gnn_W", "L0_gnn_a", "L1_gnn_W1", "L1_gnn_b1",
        "L1_gnn_g_mlp", "L1_gnn_be_mlp", "L1_gnn_W2", "L1_gnn_b2", "L1_gnn_g_out", "L1_gnn_be_out"]


def kernel(**inputs):
    import numpy as _np
    import concourse.bacc as _bacc
    from concourse import mybir as _mybir
    from concourse.bass_utils import run_bass_kernel_spmd as _run

    nc = _bacc.Bacc("TRN2", target_bir_lowering=False, num_devices=1)
    arrays, args = {}, []
    for name in _INS:
        t = _np.ascontiguousarray(inputs[name])
        arrays[f"in_{name}"] = t
        args.append(nc.dram_tensor(f"in_{name}", t.shape, _mybir.dt.from_np(t.dtype), kind="ExternalInput").ap())
    args.append(nc.dram_tensor("out_nodes", (NODES, D), F32, kind="ExternalOutput").ap())
    build(nc, *args)
    r = _run(nc, [arrays], core_ids=[0])
    return r.results[0]["out_nodes"]
```

```python
from contextlib import ExitStack

import concourse.bass as bass
from concourse import mybir

ALU = mybir.AluOpType
ACT = mybir.ActivationFunctionType
AX = mybir.AxisListType
F32 = mybir.dt.float32
I32 = mybir.dt.int32
I16 = mybir.dt.int16
BF16 = mybir.dt.bfloat16
RED = bass.bass_isa.ReduceOp

P = 128
D = 128
NODES = 6250
EDGES = 200000
LAYERS = 3
BLOCKS = -(-NODES // P)
LAST = NODES - (BLOCKS - 1) * P
COLS = BLOCKS * P
CHUNK = 512
CHUNKS = -(-COLS // CHUNK)
BY_CHUNK = CHUNK // P
SPLIT_AT = CHUNKS // 2 * BY_CHUNK
U = 11
GROUP = P * U
GROUPS = EDGES // GROUP
PAIRS = GROUPS // 2
ROUNDS = (PAIRS - 1) // 2
PICKED = (1, 2, 3)
TAIL = EDGES - GROUPS * GROUP
TAIL_AT = GROUPS * GROUP
ROW = D + 2
SUM = D + 1
VAL = SUM + 2
PARTS = 3
HALF = P // 2
ONE, SCORE = D, D + 1
TABLES = 6
ACC_ROWS = 50 * P
ACC_CHUNK = 10
ATT_ROWS = 50 * P
WINDOW = 128
MAX_WINDOWS = -(-NODES // WINDOW)
LIST = 125
BY_BANK = CHUNK // ROW
FILLS = -(-BLOCKS // BY_BANK)
AGG_COLS = 50 * ROW
LN_EPS = 1e-05
BN_EPS = 1e-05
ALPHA = 0.2

assert PAIRS % 2 == 1 and EDGES % LIST == 0 and ATT_ROWS >= NODES + WINDOW and GROUPS % 2 == 0 and 0 < TAIL < P and AGG_COLS >= NODES + WINDOW and ACC_ROWS >= NODES + P


def build(nc, x, src, dst, edge_attr, edge_weight, W, a, W1, b1, g_mlp, be_mlp, W2, b2, g_out, be_out, out):
    ctx = ExitStack()
    with ctx:
        def sb(name, shape, dt=F32):
            return ctx.enter_context(nc.sbuf_tensor(name, shape, dt))

        def sem(name):
            return ctx.enter_context(nc.semaphore(name))

        att_rows = nc.dram_tensor("att_rows", (ATT_ROWS, PARTS * ROW), BF16).ap()
        gin_rows = [nc.dram_tensor(f"gin_rows{n}", (NODES, D), F32).ap() for n in range(LAYERS)]
        tables = [nc.dram_tensor(f"sums_by_src{j}", (ACC_ROWS, SUM), F32).ap() for j in range(TABLES)]
        src_list = nc.dram_tensor("src_16_bits", (EDGES,), I16).ap()
        dst_list = nc.dram_tensor("dst_16_bits", (EDGES,), I16).ap()

        agg = sb("agg", [P, AGG_COLS])
        nodes = sb("nodes", [P, BLOCKS, D])
        work = sb("work", [P, AGG_COLS])
        att = sb("att", [P, BLOCKS, ROW])
        gath = sb("gath", [P, 2, U, VAL])
        attr = sb("attr", [P, 2, U, D])
        val = gath
        sent = sb("sent", [P, 2, U, VAL])
        src_row = sb("src_row", [P, 2, GROUP], I16)
        dst_row = sb("dst_row", [P, 2, GROUP], I16)
        lo = sb("lo", [P, GROUP], I16)
        lo_hot = [sb(f"lo_hot{s}", [P, GROUP], BF16) for s in range(2)]
        dst_hot = [sb(f"dst_hot{s}", [P, GROUP], BF16) for s in range(2)]
        hot = sb("hot", [P, U, WINDOW])
        window = sb("window", [P, 2, PARTS, ROW], BF16)
        match = attr
        zeros = sb("zeros", [1, P + CHUNK], BF16)
        dst_rel = sb("dst_rel", [P, GROUPS + 1, U])
        src_all = gath[:, :, :, :].rearrange("p s k c -> p (s k c)").bitcast(I32)
        dst_all = sent[:, :, :, :].rearrange("p s k c -> p (s k c)").bitcast(I32)
        DST_AT = BLOCKS * ROW - (GROUPS + 1) * U
        dst_cols = (att[:, :, :].rearrange("p b c -> p (b c)")[:, DST_AT:BLOCKS * ROW].bitcast(I32)
                    .rearrange("p (g k) -> p g k", k=U))
        src_i = sb("src_i", [P, 2, U], I32)
        wgt = sb("wgt", [P, 2, U])
        src_f = sb("src_f", [P, 2, U])
        hi = sb("hi", [P, U], I32)
        hi_f = sb("hi_f", [P, U])
        picked = sb("picked", [P, U, BLOCKS])
        power_bits = sb("power_bits", [P, 1], I32)
        powers = sb("powers", [P, 2])
        bounds = sb("bounds", [P, 2])
        before = sb("before", [P, 2, U])
        to_own = sb("to_own", [P, 2, U])
        moved = sb("moved", [P, U])
        sum_idx = sb("sum_idx", [P, 2, U], I32)
        s_src = sb("s_src", [P, U])
        pick_f = sb("pick_f", [P, GROUPS])
        spread_src = sb("spread_src", [P, len(PICKED), P])
        ones = sb("ones", [P, P])
        src_rel = sb("src_rel", [P, len(PICKED), P], I16)
        z = sb("z", [P, U])
        zl = sb("zl", [P, U])
        ez = sb("ez", [P, U])
        e = sb("e", [P, U])
        s1 = sb("s1", [P, BLOCKS])
        s1_parts = sb("s1_parts", [P, PARTS, BLOCKS], BF16)
        stat = sb("stat", [P, 8, BLOCKS])
        ident = sb("ident", [P, P])
        iota_row = sb("iota_row", [P, P])
        iota_p = sb("iota_p", [P, 1])
        own_row = sb("own_row", [P, 1])
        shifts = sb("shifts", [P, MAX_WINDOWS + 1])
        dmax = sb("dmax", [P, GROUPS + 1])
        dneg = sb("dneg", [P, GROUPS + 1])
        gmax = sb("gmax", [P, GROUPS + 1])
        gneg = sb("gneg", [P, GROUPS + 1])
        win_f = sb("win_f", [1, 4, GROUPS + 1])
        win_slot = sb("win_slot", [1, 4, GROUPS + 1])
        base_p = sb("base_p", [P, GROUPS + 1])
        slot_first_i = sb("slot_first_i", [1, GROUPS + 1], I32)
        base_i = sb("base_i", [1, GROUPS + 1], I32)
        span_i = sb("span_i", [1, GROUPS + 1], I32)
        count_i = sb("count_i", [1, GROUPS + 1], I32)
        first_i = sb("first_i", [1, GROUPS + 1], I32)
        W_sb = sb("W_sb", [P, ROW])
        a_sb = sb("a_sb", [P, 2])
        W_turned = hot[:, 0, :]
        ln = sb("ln", [P, BLOCKS, 6])
        ln_mv = sb("ln_mv", [P, BLOCKS, 2])
        W1_sb = sb("W1_sb", [P, LAYERS, D])
        W2_sb = sb("W2_sb", [P, LAYERS, D])
        par = sb("par", [P, 6, LAYERS])
        bn = sb("bn", [P, CHUNKS, 6])
        bn_mv = sb("bn_mv", [P, 2])
        bn_t = sb("bn_t", [P, 6])
        ps = ctx.enter_context(nc.psum_tensor("ps", [P, 8, CHUNK], F32))

        PER = CHUNK // VAL
        BANKS = -(-U // PER)
        LEFT = (CHUNK - PER * ROW) // BLOCKS

        def given(p, k):
            return ps[0:p, k // PER, k % PER * ROW:(k % PER + 1) * ROW]

        def summed(p, k):
            return ps[0:p, BANKS + k // PER, k % PER * VAL:(k % PER + 1) * VAL]

        def score_bank(k):
            return min(k // LEFT, BANKS - 1)

        def scores(p, k):
            bank = score_bank(k)
            at = (U - (BANKS - 1) * PER if bank == BANKS - 1 else PER) * ROW + (k - bank * LEFT) * BLOCKS
            return ps[0:p, bank, at:at + BLOCKS]

        def spans(u):
            full = u // PER
            return ([(0, full, PER)] if full else []) + ([(full, 1, u % PER)] if u % PER else [])

        flat = work[:, :]
        two_parts = agg[:, 0:BLOCKS * ROW].bitcast(BF16).rearrange("p (b t c) -> p b t c", t=2, c=ROW)
        IN_GATH = 2 * U * VAL * 2 // ROW
        PIECES = [(b, min(b + IN_GATH // 4, BLOCKS)) for b in range(0, BLOCKS, IN_GATH // 4)]

        ROWS_STORED = 16 * (1 + 2 * len(PIECES))

        def last_part(begin, end):
            t, at = (gath, begin) if end <= IN_GATH else (sent, begin - IN_GATH // 4 * 4)
            return (t[:, :, :, :].rearrange("p s k c -> p (s k c)").bitcast(BF16)[:, at * ROW:(at + end - begin) * ROW]
                    .rearrange("p (b c) -> p b c", c=ROW))

        first_parts = att[:, :, :].rearrange("p b c -> p (b c)").bitcast(BF16)[:, 0:2 * COLS].rearrange("p (t b d) -> p t b d", t=2, d=D)

        def in_places(places):
            views, at = [], 0
            for t, blocks in places:
                n = min(blocks, BLOCKS - at)
                views.append((at, at + n, t.bitcast(BF16)[:, 0:n * P].rearrange("p (b d) -> p b d", d=P)))
                at += n
            assert at == BLOCKS
            return views

        third_part = in_places(((sent[:, :, :, :].rearrange("p s k c -> p (s k c)"), 2 * U * VAL * 2 // P), (lo[:, :], U)))
        node_hot = in_places(((src_row[:, :, :].rearrange("p s e -> p (s e)"), 2 * U), (dst_row[:, :, :].rearrange("p s e -> p (s e)"), 2 * U),
                              (lo_hot[0][:, :], U)))

        def block_in(views, b):
            return next(view[:, b - begin, :] for begin, end, view in views if begin <= b < end)

        def part_of(t, b):
            return first_parts[:, t, b, :] if t < 2 else block_in(third_part, b)

        s_nodes, s_dsts, s_small = sem("nodes_loaded"), sem("dsts_loaded"), sem("weights_loaded")
        s_attw = sem("attention_weights_loaded")
        s_const, s_pad, s_zero, s_zeroed = sem("constants"), sem("nodes_padded"), sem("zeros_set"), sem("tables_zeroed")
        s_step = sem("vector_step")
        s_w_turned, s_w_kept = sem("w_by_pe"), sem("w_kept")
        s_att_row, s_gin_row = sem("att_rows_stored"), [sem(f"gin_rows_stored{n}") for n in range(LAYERS)]
        s_extent, s_extents = sem("extents_by_partition"), sem("extents_of_groups")
        s_windows = sem("windows_listed")
        s_var, s_std, s_scaled = sem("variance_ready"), sem("deviation_ready"), sem("scale_ready")
        s_normed = [sem(f"normed{n}") for n in range(2)]
        TURNS = ["att_in", "gin_in"] + [f"gin_out{n}" for n in range(LAYERS)]
        s_turned = {t: sem(f"turned_{t}") for t in TURNS}
        s_copied = {t: sem(f"turned_copied_{t}") for t in TURNS}
        s_h, s_h_kept, s_att_ready = sem("h_product"), sem("h_kept"), sem("att_ready")
        s_cols = [sem(f"edge_columns_loaded{s}") for s in range(2)]
        s_lists, s_narrow, s_listed = sem("lists_loaded"), sem("lists_in_16_bits"), sem("lists_stored")
        s_window = [sem(f"window_loaded{s}") for s in range(2)]
        s_dsthot = [sem(f"dst_hot_ready{s}") for s in range(2)]
        s_given = [sem(f"window_given{s}") for s in range(2)]
        s_srcf, s_hi, s_lo, s_lohot = sem("src_f_ready"), sem("hi_ready"), sem("lo_ready"), sem("lo_hot_ready")
        s_match, s_before, s_later = sem("match_ready"), sem("before_ready"), sem("later_ready")
        s_own, s_moved, s_idx = sem("to_own_ready"), sem("moved_ready"), sem("sum_idx_ready")
        s_hif, s_score, s_ssrc = sem("hi_f_ready"), sem("scores_by_block"), sem("s_src_ready")
        s_z, s_zl, s_ez, s_e = sem("z_ready"), sem("leaky_ready"), sem("exp_ready"), sem("e_ready")
        s_val = [sem(f"val_ready{s}") for s in range(2)]
        s_sums, s_sent = sem("equal_sources_summed"), [sem(f"sent_ready{s}") for s in range(2)]
        s_added = [sem(f"added_to_table{j}") for j in range(TABLES)]
        s_table, s_tabled = sem("first_table_loaded"), sem("table_summed")
        s_staged = [sem(f"table_loaded{n}") for n in range(2)]
        s_elu, s_expm = sem("elu_in_ready"), sem("elu_exp_ready")
        s_g = [[sem(f"gathered{n}{s}") for s in range(2)] for n in range(LAYERS)]
        s_idxs = [[sem(f"src_loaded{n}{s}") for s in range(2)] for n in range(LAYERS)]
        s_attr = [[sem(f"attr_loaded{n}{s}") for s in range(2)] for n in range(LAYERS)]
        s_raw = [[sem(f"message_summed{n}{s}") for s in range(2)] for n in range(LAYERS)]
        s_msg = [[sem(f"message_ready{n}{s}") for s in range(2)] for n in range(LAYERS)]
        s_free = [[sem(f"message_used{n}{s}") for s in range(2)] for n in range(LAYERS)]
        s_hot = [sem(f"hot_ready{n}") for n in range(LAYERS)]
        s_win = [sem(f"window_summed{n}") for n in range(LAYERS)]
        s_agg = [sem(f"window_added{n}") for n in range(LAYERS)]
        s_mm = sem("product")
        s_mmk = sem("product_kept")
        s_mmv = sem("product_kept_by_dve")
        s_bnv = sem("bn_var")
        s_bns = sem("bn_std")
        s_bnp = sem("bn_scale")
        s_act = sem("normed_kept")
        s_summed = sem("all_messages_summed")
        s_part, s_rest = sem("part_ready"), sem("rest_ready")
        s_diag, s_spread = sem("sources_on_diagonal"), sem("sources_spread")
        s_rel, s_picked = sem("sources_relative"), sem("picked_message_ready")
        s_pick = [sem(f"rows_picked{h}") for h in range(2)]
        s_nodehot = [sem(f"node_hot_ready{h}") for h in range(2)]
        s_out = sem("out_stored")
        s_pool = sem("pool_may_go")

        block = ctx.enter_context(nc.Block())

        def edges(ap, i, slot):
            at = (2 * i + slot) * GROUP
            return ap[at:at + GROUP] if isinstance(i, int) else ap[bass.ds(at, GROUP)]

        def adds(i, slot, k, j):
            return 16 * (len(range(j, 2 * U, TABLES)) * i + len(range(j, U * slot + k, TABLES)))

        def narrow(t):
            return t[0:LIST, :, :].rearrange("p s e -> p (s e)")[:, 0:EDGES // LIST]

        def window_at(base, w):
            return nc.s_assert_within(base + w * WINDOW, 0, NODES - 1, skip_runtime_bounds_check_because="a window begins at a destination or before one")

        def by_block(t):
            return t.rearrange("p (b d) -> p b d", d=D)

        def chunks_before(n, m):
            return (2 * n + m) * CHUNKS

        def sums_of(begin, end):
            return agg[:, begin * SUM:end * SUM].rearrange("p (b c) -> p b c", c=SUM)

        def stage_of(n, blocks):
            at = n % 2 * (AGG_COLS // 2)
            return work[:, at:at + blocks * SUM].rearrange("p (b c) -> p b c", c=SUM)

        HALVES = ((0, SPLIT_AT), (SPLIT_AT, BLOCKS))

        def kept_by_dve(m, c):
            return m == 1 and c % 3 != 1

        def wait_kept(eng, n, m, c):
            by_dve = kept_by_dve(m, c)
            count = sum(kept_by_dve(k, t) == by_dve for k in range(2) for t in range(CHUNKS)) * n
            count += sum(kept_by_dve(k, t) == by_dve for k in range(m + 1) for t in range(CHUNKS) if k < m or t <= c)
            eng.wait_ge(s_mmv if by_dve else s_mmk, count)

        def rows_of(t, c):
            if c == CHUNKS - 1:
                return t[0:LAST, c * CHUNK:c * CHUNK + D]
            return t[:, c * CHUNK:(c + 1) * CHUNK].rearrange("p (b d) -> p b d", d=D)

        NO_PICKS = len(PICKED) + 1

        def pick_no(n, q, j):
            return n * len(PICKED) * ROUNDS + len(PICKED) * q + j

        def round_no(n, q):
            return n * ROUNDS + q + 1

        def pair_of(q, j):
            return 2 * q + 1 + j // 2

        def group_of(q, j):
            return 2 + 4 * q + j

        def column(g):
            return slice(g, g + 1) if isinstance(g, int) else bass.ds(g, 1)

        def tiles_gathered(j):
            return U - 1 if j in PICKED else U

        def gathered(q, j):
            of_slot = range(j % 2, 4, 2)
            return U + sum(tiles_gathered(t) for t in of_slot) * q + sum(tiles_gathered(t) for t in of_slot if t <= j)

        def width(c):
            return min(CHUNK, NODES - c * CHUNK)

        def blocks_of(c):
            return [(b, LAST if b == BLOCKS - 1 else P) for b in range(4 * c, min(4 * c + 4, BLOCKS))]

        @block.sync
        def _(sp):
            def store_rows(to, ready, before, done):
                for c in range(CHUNKS):
                    sp.wait_ge(ready, before + c + 1)
                    rows = to[c * CHUNK:min((c + 1) * CHUNK, NODES)]
                    sp.dma_start(rows if c == CHUNKS - 1 else rows.rearrange("(b p) d -> p b d", p=P),
                                 rows_of(flat, c)).then_inc(done, 16)

            sp.wait_ge(s_pad, 1)
            whole = (BLOCKS - 1) * P
            sp.dma_start(nodes[:, 0:BLOCKS - 1, :], x[0:whole].rearrange("(b p) d -> p b d", p=P)).then_inc(s_nodes, 16)
            sp.dma_start(nodes[0:LAST, BLOCKS - 1, :], x[whole:NODES]).then_inc(s_nodes, 16)
            sp.dma_start(W_sb[:, 0:D], W).then_inc(s_attw, 16)
            with nc.allow_non_contiguous_dma(reason="two columns of weights"):
                sp.dma_start(a_sb[:, :], a.rearrange("o (j n) -> n (o j)", n=D)).then_inc(s_attw, 16)
            sp.dma_start(W1_sb[:, :, :], W1.rearrange("l d n -> d l n")).then_inc(s_small, 16)
            sp.dma_start(W2_sb[:, :, :], W2.rearrange("l d n -> d l n")).then_inc(s_small, 16)
            with nc.allow_non_contiguous_dma(reason="six small parameters by feature"):
                for n, t in enumerate((b1, g_mlp, be_mlp, b2, g_out, be_out)):
                    sp.dma_start(par[:, n, :], t.rearrange("l d -> d l")).then_inc(s_small, 16)
            sp.dma_start(src_all[0:LIST, 0:EDGES // LIST], src.rearrange("(p n) -> p n", p=LIST)).then_inc(s_lists, 16)
            sp.dma_start(dst_all[0:LIST, 0:EDGES // LIST], dst.rearrange("(p n) -> p n", p=LIST)).then_inc(s_lists, 16)
            sp.dma_start(dst_cols[:, 0:GROUPS, :], dst[0:TAIL_AT].rearrange("(g p k) -> p g k", p=P, k=U)).then_inc(s_dsts, 16)
            sp.dma_start(dst_cols[0:TAIL, GROUPS, 0:1], dst[TAIL_AT:EDGES].rearrange("(p k) -> p k", k=1)).then_inc(s_dsts, 16)
            sp.wait_ge(s_zero, 1)
            none = attr[:, 0, :, :].rearrange("p k d -> p (k d)")[:, 0:ACC_CHUNK * SUM]
            for t in tables:
                v = t.rearrange("(p q r) c -> q p (r c)", p=P, r=ACC_CHUNK)
                for q in range(ACC_ROWS // P // ACC_CHUNK):
                    sp.dma_start(v[q], none).then_inc(s_zeroed, 16)
            sp.wait_ge(s_narrow, 2)
            sp.dma_start(src_list.rearrange("(p n) -> p n", p=LIST), narrow(src_row)).then_inc(s_listed, 16)
            sp.dma_start(dst_list.rearrange("(p n) -> p n", p=LIST), narrow(dst_row)).then_inc(s_listed, 16)
            rows = att_rows[0:COLS].rearrange("(b p) c -> p b c", p=P)
            for n, (begin, end) in enumerate(PIECES):
                sp.wait_ge(s_att_ready, 2 * n + 1)
                sp.dma_start(rows[:, begin:end, 0:2 * ROW], two_parts[:, begin:end, :, :].rearrange("p b t c -> p b (t c)")).then_inc(s_att_row, 16)
                sp.wait_ge(s_att_ready, 2 * n + 2)
                sp.dma_start(rows[:, begin:end, 2 * ROW:PARTS * ROW], last_part(begin, end)).then_inc(s_att_row, 16)
            sp.dma_start(att_rows[COLS:ATT_ROWS], none[:, 0:PARTS * ROW // 2].bitcast(BF16)).then_inc(s_att_row, 16)
            sp.wait_ge(s_listed, 32)
            sp.wait_ge(s_windows, 1)

            def listed(t, g, most):
                return sp.value_load(t[0:1, g], min_val=0, max_val=most)

            def load_columns(i, slot, p, u, part, g):
                sp.wait_ge(s_val[slot], i)
                for to, of in ((src_i, src), (wgt, edge_weight)):
                    sp.dma_start(to[0:p, slot, 0:u], part(of).rearrange("(p k) -> p k", k=u)).then_inc(s_cols[slot], 16)
                for to, of in ((src_row, src_list), (dst_row, dst_list)):
                    sp.dma_start(to[:, slot, 0:p * u], part(of).partition_broadcast(P)).then_inc(s_cols[slot], 16)
                base, first, count = (listed(base_i, g, NODES - 1), listed(slot_first_i, g, GROUPS * MAX_WINDOWS),
                                      listed(count_i, g, MAX_WINDOWS))
                if isinstance(i, int) and i == 0:
                    sp.wait_ge(s_att_row, ROWS_STORED)
                with sp.Fori(0, count) as w:
                    sp.wait_ge(s_given[slot], first + w)
                    sp.dma_start(window[:, slot, :, :].rearrange("p t c -> p (t c)"), att_rows[bass.ds(window_at(base, w), WINDOW), :]).then_inc(s_window[slot], 16)

            for slot in range(2):
                load_columns(0, slot, P, U, lambda of: edges(of, 0, slot), slice(slot, slot + 1))
            with sp.Fori(1, PAIRS) as i:
                for slot in range(2):
                    load_columns(i, slot, P, U, lambda of: edges(of, i, slot), bass.ds(2 * i + slot, 1))
            load_columns(PAIRS, 0, TAIL, 1, lambda of: of[TAIL_AT:EDGES], slice(GROUPS, GROUPS + 1))

            for j in range(TABLES):
                sp.wait_ge(s_added[j], adds(PAIRS, 0, 1, j))
            staged = 0
            for begin, end in HALVES:
                for n, t in enumerate(tables):
                    if n == 0:
                        to, done = sums_of(begin, end), s_table
                    else:
                        to, done = stage_of(staged, end - begin), s_staged[staged % 2]
                        if staged >= 2:
                            sp.wait_ge(s_tabled, staged - 1)
                        staged += 1
                    sp.dma_start(to, t[0:COLS].rearrange("(b p) c -> p b c", p=P)[:, begin:end, :]).then_inc(done, 16)
            store_rows(gin_rows[0], s_normed[1], 0, s_gin_row[0])

            sp.wait_ge(s_sums, GROUPS + 1)
            for n in range(LAYERS):
                def load_group(i, slot, p, u, part, part_attr):
                    sp.wait_ge(s_raw[n][slot], i)
                    sp.dma_start(src_i[0:p, slot, 0:u], part(src).rearrange("(p k) -> p k", k=u)).then_inc(s_idxs[n][slot], 16)
                    sp.dma_start(attr[0:p, slot, 0:u, :], part_attr.rearrange("(p k) d -> p k d", k=u)).then_inc(s_attr[n][slot], 16)

                for slot in range(2):
                    load_group(0, slot, P, U, lambda of: edges(of, 0, slot), edge_attr[slot * GROUP:(slot + 1) * GROUP, :])
                with sp.Fori(0, ROUNDS) as q:
                    for j in range(4):
                        if (j + 2) % 4 in PICKED:
                            sp.wait_ge(s_pick[1], pick_no(n, q, j - 2 if j >= 2 else j + 2 - len(PICKED)) + NO_PICKS)
                        i, slot = pair_of(q, j), j % 2
                        load_group(i, slot, P, U, lambda of: of[bass.ds(group_of(q, j) * GROUP, GROUP)],
                                   edge_attr[bass.ds(group_of(q, j) * GROUP, GROUP), :])
                load_group(PAIRS, 0, TAIL, 1, lambda of: of[TAIL_AT:EDGES], edge_attr[TAIL_AT:EDGES, :])
                to, done = (gin_rows[n + 1], s_gin_row[n + 1]) if n + 1 < LAYERS else (out, s_out)
                store_rows(to, s_copied[f"gin_out{n}"], 0, done)
            for n in range(LAYERS):
                sp.wait_ge(s_gin_row[n], 16 * CHUNKS)
            sp.wait_ge(s_out, 16 * CHUNKS)

        @block.gpsimd
        def _(pool):
            pool.memset(ident[:, :], 1.0).then_inc(s_const, 1)
            pool.wait_ge(s_const, 1)
            pool.affine_select(out=ident[:, :], in_=ident[:, :], compare_op=ALU.is_equal, fill=0.0,
                               base=0, pattern=[[-1, P]], channel_multiplier=1).then_inc(s_const, 1)
            pool.iota(iota_row[:, :], [[1, P]], base=0, channel_multiplier=0,
                      allow_small_or_imprecise_dtypes=True).then_inc(s_const, 1)
            pool.iota(iota_p[:, :], [[1, 1]], base=0, channel_multiplier=1,
                      allow_small_or_imprecise_dtypes=True).then_inc(s_const, 1)
            pool.iota(own_row[:, :], [[1, 1]], base=NODES, channel_multiplier=1,
                      allow_small_or_imprecise_dtypes=True).then_inc(s_const, 1)
            pool.iota(shifts[:, :], [[WINDOW, MAX_WINDOWS + 1]], base=0, channel_multiplier=0,
                      allow_small_or_imprecise_dtypes=True).then_inc(s_const, 1)
            pool.wait_ge(s_extent, 1)
            pool.partition_all_reduce(gmax[:, :], dmax[:, :], P, RED.max).then_inc(s_extents, 1)
            pool.partition_all_reduce(gneg[:, :], dneg[:, :], P, RED.max).then_inc(s_extents, 1)

            def add_sums(i, slot, p, u):
                pool.wait_ge(s_sent[slot], BANKS * (i + 1))
                pool.wait_ge(s_idx, 2 * i + slot + 1)
                pool.wait_ge(s_zeroed, 16 * TABLES * (ACC_ROWS // P // ACC_CHUNK))
                for k in range(u):
                    j = (U * slot + k) % TABLES
                    pool.wait_ge(s_added[j], adds(i, slot, k, j))
                    pool.sem_inc(s_pool, 1)
                    pool.indirect_dma_start(
                        out=tables[j],
                        out_offset=bass.IndirectOffsetOnAxis(ap=sum_idx[0:p, slot, k:k + 1], axis=0),
                        in_=sent[0:p, slot, k, 0:SUM], in_offset=None, compute_op=ALU.add,
                    ).then_inc(s_added[j], 16)

            for slot in range(2):
                add_sums(0, slot, P, U)
            with pool.Fori(1, PAIRS) as i:
                for slot in range(2):
                    add_sums(i, slot, P, U)
            add_sums(PAIRS, 0, TAIL, 1)

            for n in range(LAYERS):
                def gather_group(i, slot, p, u):
                    pool.wait_ge(s_idxs[n][slot], 16 * (i + 1))
                    pool.wait_ge(s_free[n][slot], i)
                    pool.wait_ge(s_gin_row[n], 16 * CHUNKS)
                    pool.sem_inc(s_pool, 1)
                    for k in range(u):
                        pool.indirect_dma_start(
                            out=gath[0:p, slot, k, 0:D], out_offset=None, in_=gin_rows[n],
                            in_offset=bass.IndirectOffsetOnAxis(ap=src_i[0:p, slot, k:k + 1], axis=0),
                        ).then_inc(s_g[n][slot], 16)

                for slot in range(2):
                    gather_group(0, slot, P, U)
                with pool.Fori(0, ROUNDS) as q:
                    for j in range(4):
                        gather_group(pair_of(q, j), j % 2, P, tiles_gathered(j))
                gather_group(PAIRS, 0, TAIL, 1)

        @block.scalar
        def _(act):
            act.wait_ge(s_w_turned, 1)
            act.activation(W_turned, ps[:, 7, 0:D], ACT.Copy).then_inc(s_w_kept, 1)
            act.wait_ge(s_w_turned, 2)
            act.activation(W_sb[:, D:ROW], ps[:, 7, 0:2], ACT.Copy).then_inc(s_w_kept, 1)
            act.wait_ge(s_var, 1)
            act.activation(stat[:, 4, :], stat[:, 3, :], ACT.Sqrt).then_inc(s_std, 1)
            for c in range(CHUNKS):
                act.wait_ge(s_turned["att_in"], c + 1)
                n = min(CHUNK, COLS - c * CHUNK)
                act.activation(agg[:, c * CHUNK:c * CHUNK + n], ps[:, 6 + c % 2, 0:n], ACT.Relu).then_inc(s_copied["att_in"], 1)
            act.wait_ge(s_extent, 1)
            for c in range(FILLS):
                act.wait_ge(s_h, c + 1)
                nb = min(BY_BANK, BLOCKS - c * BY_BANK)
                act.activation(att[:, BY_BANK * c:BY_BANK * c + nb, :],
                               ps[:, 4 + c % 2, 0:nb * ROW].rearrange("p (b d) -> p b d", d=ROW), ACT.Copy).then_inc(s_h_kept, 1)

            def weigh(i, slot, p, u):
                act.wait_ge(s_zl, 2 * i + slot + 1)
                act.activation(ez[0:p, 0:u], zl[0:p, 0:u], ACT.Exp, scale=-1.0).then_inc(s_ez, 1)

            def keep_sums(i, slot, p, u):
                act.wait_ge(s_sums, 2 * i + slot + 1)
                if not (isinstance(i, int) and i == 0):
                    for j in range(TABLES):
                        act.wait_ge(s_added[j], adds(i - 1, slot, U, j))
                if u == U:
                    for b in range(BANKS):
                        k, n = PER * b, min(PER, U - PER * b)
                        act.activation(sent[0:p, slot, k:k + n, :], ps[0:p, BANKS + b, 0:n * VAL].rearrange("p (k c) -> p k c", c=VAL),
                                       ACT.Copy).then_inc(s_sent[slot], 1)
                else:
                    act.activation(sent[0:p, slot, 0, :], summed(p, 0), ACT.Copy).then_inc(s_sent[slot], BANKS)

            def turn_of(i):
                weigh(i, 1, P, U)
                keep_sums(i, 0, P, U)
                weigh(i + 1, 0, P, U)
                keep_sums(i, 1, P, U)

            weigh(0, 0, P, U)
            turn_of(0)
            with act.Fori(1, PAIRS - 1) as i:
                turn_of(i)
            weigh(PAIRS - 1, 1, P, U)
            keep_sums(PAIRS - 1, 0, P, U)
            weigh(PAIRS, 0, TAIL, 1)
            keep_sums(PAIRS - 1, 1, P, U)
            keep_sums(PAIRS, 0, TAIL, 1)

            for n, (begin, end) in enumerate(HALVES):
                act.wait_ge(s_elu, n + 1)
                act.activation(att[:, begin:end, 0:D], sums_of(begin, end)[:, :, 0:D], ACT.Exp).then_inc(s_expm, 1)
                act.wait_ge(s_var, n + 2)
                act.activation(stat[:, 4, begin:end], stat[:, 3, begin:end], ACT.Sqrt).then_inc(s_std, 1)
                if n == 0:
                    act.wait_ge(s_scaled, 1)
                    for b in range(begin, end):
                        ins = act.activation(flat[:, b * D:(b + 1) * D], nodes[:, b, :], ACT.Relu, bias=stat[:, 6, b:b + 1],
                                             scale=stat[:, 5, b:b + 1])
                        if b % BY_CHUNK == BY_CHUNK - 1:
                            ins.then_inc(s_normed[1], 1)
            for c in range(CHUNKS):
                act.wait_ge(s_turned["gin_in"], c + 1)
                w = width(c)
                act.activation(agg[:, c * CHUNK:c * CHUNK + w], ps[:, 6 + c % 2, 0:w], ACT.Copy).then_inc(s_copied["gin_in"], 1)

            act.wait_ge(s_small, 128)
            act.sem_inc(s_picked, NO_PICKS)
            for n in range(LAYERS):
                def messages(i, slot, p, u):
                    act.wait_ge(s_raw[n][slot], i + 1)
                    act.activation(gath[0:p, slot, 0:u, 0:D], gath[0:p, slot, 0:u, 0:D], ACT.Relu).then_inc(s_msg[n][slot], 1)

                rows = by_block(flat[:, 0:COLS])
                act.wait_ge(s_normed[1] if n == 0 else s_copied[f"gin_out{n - 1}"], CHUNKS)
                act.activation(first_parts[:, 0], rows, ACT.Copy).then_inc(s_part, 1)
                act.wait_ge(s_rest, 2 * n + 1)
                act.activation(first_parts[:, 1], rows, ACT.Copy).then_inc(s_part, 1)
                messages(0, 0, P, U)
                act.wait_ge(s_rest, 2 * n + 2)
                for begin, end, view in third_part:
                    ins = act.activation(view, rows[:, begin:end, :], ACT.Copy)
                ins.then_inc(s_part, 1)
                messages(0, 1, P, U)
                with act.Fori(0, ROUNDS) as q:
                    for j in range(4):
                        i, slot = pair_of(q, j), j % 2
                        if j in PICKED:
                            act.wait_ge(s_pick[1], pick_no(n, q, j) + NO_PICKS)
                            act.wait_ge(s_free[n][slot], i)
                            act.activation(gath[:, slot, U - 1, 0:D], ps[:, j, 0:D], ACT.Relu).then_inc(s_picked, 1)
                        messages(i, slot, P, tiles_gathered(j))
                messages(PAIRS, 0, TAIL, 1)

                def keep(m, c):
                    to, w = (flat, agg)[m], width(c)
                    act.wait_ge(s_mm, chunks_before(n, m) + c + 1)
                    act.activation(to[:, c * CHUNK:c * CHUNK + w], ps[:, 4 + c % 4, 0:w], ACT.Identity,
                                   bias=par[:, 3 * m, n:n + 1]).then_inc(s_mmk, 1)

                def normalise(m, c):
                    to, w = (flat, agg)[m], width(c)
                    act.activation(to[:, c * CHUNK:c * CHUNK + w], to[:, c * CHUNK:c * CHUNK + w],
                                   ACT.Identity if m == 1 and n == LAYERS - 1 else ACT.Relu,
                                   bias=bn_t[:, 5:6], scale=bn_t[:, 3:4]).then_inc(s_act, 1)

                for c in range(CHUNKS):
                    keep(0, c)
                for m in range(2):
                    act.wait_ge(s_bnv, 2 * n + m + 1)
                    act.activation(bn_t[:, 1:2], bn_t[:, 0:1], ACT.Sqrt).then_inc(s_bns, 1)
                    act.wait_ge(s_bnp, 2 * n + m + 1)
                    for c in range(CHUNKS):
                        normalise(m, c)
                        if m == 0 and c >= 2 and not kept_by_dve(1, c - 2):
                            keep(1, c - 2)
                    if m == 0:
                        for c in range(CHUNKS - 2, CHUNKS):
                            if not kept_by_dve(1, c):
                                keep(1, c)

        @block.vector
        def _(vec):
            steps = [0]

            def link(ins):
                steps[0] += 1
                ins.then_inc(s_step, 1)
                vec.wait_ge(s_step, steps[0])

            def moments(begin, end):
                for b in range(begin, end):
                    ins = vec.bn_stats(ln[:, b, :], nodes[:, b, :])
                link(ins)
                for b in range(begin, end):
                    ins = vec.bn_aggr(ln_mv[:, b, :], ln[:, b, :])
                link(ins)
                vec.tensor_scalar(stat[:, 3, begin:end], ln_mv[:, begin:end, 1], LN_EPS, None, ALU.add).then_inc(s_var, 1)

            vec.memset(nodes[96:P, BLOCKS - 1, :], 0.0).then_inc(s_pad, 1)
            vec.memset(attr[:, 0, :, :], 0.0).then_inc(s_zero, 1)
            vec.memset(dmax[:, :], 0.0)
            vec.memset(dneg[:, :], -float(NODES))
            vec.memset(zeros[:, :], 0.0)
            vec.memset(ones[:, :], 1.0)
            vec.memset(agg[:, NODES:AGG_COLS], 0.0)
            link(vec.memset(dst_rel[:, :, :], 0.0))
            vec.wait_ge(s_nodes, 32)
            moments(0, BLOCKS)
            vec.wait_ge(s_std, 1)
            link(vec.reciprocal(stat[:, 5, :], stat[:, 4, :]))
            for b in range(BLOCKS):
                ins = vec.tensor_scalar(flat[:, b * D:(b + 1) * D], nodes[:, b, :], ln_mv[:, b, 0:1], stat[:, 5, b:b + 1],
                                        ALU.subtract, ALU.mult)
                if b % BY_CHUNK == BY_CHUNK - 1 or b == BLOCKS - 1:
                    ins.then_inc(s_normed[0], 1)
            vec.wait_ge(s_dsts, 32)
            vec.tensor_copy(dst_rel[:, 0:GROUPS, :], dst_cols[:, 0:GROUPS, :])
            link(vec.tensor_copy(dst_rel[0:TAIL, GROUPS, 0:1], dst_cols[0:TAIL, GROUPS, 0:1]))
            vec.tensor_reduce(dmax[:, 0:GROUPS], dst_rel[:, 0:GROUPS, :], AX.X, ALU.max)
            vec.tensor_copy(dmax[0:TAIL, GROUPS:GROUPS + 1], dst_rel[0:TAIL, GROUPS, 0:1])
            link(vec.tensor_reduce(dneg[:, 0:GROUPS], dst_rel[:, 0:GROUPS, :], AX.X, ALU.min))
            vec.tensor_scalar(dneg[:, 0:GROUPS], dneg[:, 0:GROUPS], -1.0, None, ALU.mult)
            vec.tensor_scalar(dneg[0:TAIL, GROUPS:GROUPS + 1], dst_rel[0:TAIL, GROUPS, 0:1], -1.0, None,
                              ALU.mult).then_inc(s_extent, 1)

            vec.wait_ge(s_lists, 32)
            for to, of in ((src_row, src_all), (dst_row, dst_all)):
                vec.tensor_copy(narrow(to), of[0:LIST, 0:EDGES // LIST]).then_inc(s_narrow, 1)

            vec.wait_ge(s_extents, 2)
            link(vec.tensor_tensor(dst_rel[:, :, :], dst_rel[:, :, :],
                                   gneg[:, :].unsqueeze(2).to_broadcast([P, GROUPS + 1, U]), ALU.add))
            vec.tensor_scalar(base_i[:, :], gneg[0:1, :], -1.0, None, ALU.mult)
            vec.wait_ge(s_const, 6)
            vec.tensor_scalar(base_p[:, :], gneg[:, :], -1.0, iota_p[:, 0:1], ALU.mult, ALU.add)
            link(vec.tensor_tensor(span_i[:, :], gmax[0:1, :], gneg[0:1, :], ALU.add))
            link(vec.tensor_scalar(span_i[:, :], span_i[:, :], WINDOW.bit_length() - 1, None, ALU.logical_shift_right))
            link(vec.tensor_scalar(win_f[:, 0, :], span_i[:, :], 1.0, None, ALU.add))
            vec.tensor_copy(count_i[:, :], win_f[:, 0, :])
            link(vec.memset(win_f[:, 1, :], 0.0))
            link(vec.tensor_tensor_scan(win_f[:, 2, :], win_f[:, 0, :], win_f[:, 1, :], 0.0, ALU.add, ALU.add))
            link(vec.tensor_tensor(win_f[:, 3, :], win_f[:, 2, :], win_f[:, 0, :], ALU.subtract))
            vec.tensor_scalar(first_i[:, :], win_f[:, 3, :], 1.0, None, ALU.add)
            for slot in range(2):
                of_slot = slice(slot, GROUPS + 1, 2)
                counts = win_f[:, 0, of_slot]
                link(vec.tensor_tensor_scan(win_slot[:, 0, of_slot], counts, win_f[:, 1, of_slot], 0.0, ALU.add, ALU.add))
                link(vec.tensor_tensor(win_slot[:, 1, of_slot], win_slot[:, 0, of_slot], counts, ALU.subtract))
            vec.tensor_scalar(slot_first_i[:, :], win_slot[:, 1, :], 1.0, None, ALU.add).then_inc(s_windows, 1)

            left = work[:, 0:BLOCKS * ROW].rearrange("p (b c) -> p b c", c=ROW)
            for begin, end in PIECES:
                vec.wait_ge(s_h_kept, min(end // BY_BANK + 1, FILLS))
                of, rest = att[:, begin:end, :], left[:, begin:end, :]
                link(vec.tensor_copy(s1[:, begin:end], of[:, :, ONE]))
                link(vec.memset(of[:, :, ONE:ONE + 1], 1.0))
                link(vec.tensor_copy(two_parts[:, begin:end, 0, :], of))
                link(vec.tensor_tensor(rest, of, two_parts[:, begin:end, 0, :], ALU.subtract))
                link(vec.tensor_copy(two_parts[:, begin:end, 1, :], rest))
                vec.sem_inc(s_att_ready, 1)
                link(vec.tensor_tensor(rest, rest, two_parts[:, begin:end, 1, :], ALU.subtract))
                vec.tensor_copy(last_part(begin, end), rest).then_inc(s_att_ready, 1)
            for t in range(PARTS):
                link(vec.tensor_copy(s1_parts[:, t, :], s1[:, :]))
                link(vec.tensor_tensor(s1[:, :], s1[:, :], s1_parts[:, t, :], ALU.subtract))
            vec.memset(bounds[0:HALF, 1:2], 3e38)
            vec.memset(bounds[HALF:P, 0:1], 2.0 ** -70)
            link(vec.memset(powers[:, :], 0.0))
            link(vec.tensor_scalar(moved[:, 0:1], iota_p[:, 0:1], float(HALF), -float(HALF), ALU.is_ge, ALU.mult))
            link(vec.tensor_tensor(moved[:, 0:1], moved[:, 0:1], iota_p[:, 0:1], ALU.add))
            link(vec.tensor_scalar(power_bits[:, :], moved[:, 0:1], -2.0 * 2 ** 23, (127.0 + 62.0) * 2 ** 23, ALU.mult, ALU.add))
            for half in range(2):
                of_half = slice(half * HALF, (half + 1) * HALF)
                link(vec.tensor_copy(powers[of_half, half:half + 1], power_bits[of_half, :].bitcast(F32)))
                link(vec.tensor_scalar(bounds[of_half, half:half + 1], powers[of_half, half:half + 1], 2.0, None, ALU.mult))
            vec.wait_ge(s_att_row, ROWS_STORED)
            link(vec.tensor_copy(val[:, :, :, SUM:VAL].rearrange("p s k c -> p (s k) c"), powers[:, :].unsqueeze(1).to_broadcast([P, 2 * U, 2])))
            vec.sem_inc(s_att_ready, 1)
            vec.wait_ge(s_zeroed, 16 * TABLES * (ACC_ROWS // P // ACC_CHUNK))

            vec.wait_ge(s_windows, 1)

            def listed(t, g, most):
                return vec.value_load(t[0:1, g], min_val=0, max_val=most)

            def point(i, slot, p, u, at):
                g = 2 * i + slot
                first, count = listed(slot_first_i, at, GROUPS * MAX_WINDOWS), listed(count_i, at, MAX_WINDOWS)

                def window_hot(w):
                    vec.wait_ge(s_given[slot], first + w)
                    vec.tensor_scalar(dst_hot[slot][:, 0:p * u], dst_row[:, slot, 0:p * u], shifts[:, bass.ds(w, 1)],
                                      base_p[:, at], ALU.subtract, ALU.is_equal).then_inc(s_dsthot[slot], 1)

                vec.wait_ge(s_cols[slot], 64 * (i + 1))
                window_hot(0)
                vec.wait_ge(s_lohot, g)
                vec.tensor_scalar(lo[:, 0:p * u], src_row[:, slot, 0:p * u], P - 1, None, ALU.bitwise_and).then_inc(s_lo, 1)
                if not (isinstance(i, int) and i == 0):
                    vec.wait_ge(s_score, g - 1)
                vec.wait_ge(s_lo, g + 1)
                vec.tensor_scalar(lo_hot[slot][:, 0:p * u], lo[:, 0:p * u], iota_p[:, 0:1], None, ALU.is_equal).then_inc(s_lohot, 1)

                def other_windows():
                    with vec.If(count > 1):
                        with vec.Fori(1, count) as w:
                            window_hot(w)

                return other_windows

            def attend(i, slot, p, u, point_next=None):
                g = 2 * i + slot
                src_kj = src_row[0:p, slot, 0:p * u].rearrange("p (j k) -> p k j", k=u)
                src_g = src_f[0:p, slot, 0:u]
                if not (isinstance(i, int) and i == 0):
                    vec.wait_ge(s_idx, g - 1)
                vec.tensor_copy(src_g, src_i[0:p, slot, 0:u]).then_inc(s_srcf, 1)
                if u == U:
                    vec.wait_ge(s_srcf, g + 1)
                    vec.tensor_copy(pick_f[:, column(g)], src_f[:, slot, U - 1:U])
                vec.tensor_scalar(hi[0:p, 0:u], src_i[0:p, slot, 0:u], 7, None, ALU.logical_shift_right).then_inc(s_hi, 1)
                vec.wait_ge(s_hi, g + 1)
                vec.tensor_copy(hi_f[0:p, 0:u], hi[0:p, 0:u]).then_inc(s_hif, 1)
                if not (isinstance(i, int) and i == 0):
                    vec.wait_ge(s_sums, g - 1)
                vec.wait_ge(s_srcf, g + 1)
                vec.tensor_tensor(match[0:p, slot, 0:u, 0:p], src_kj, src_g.unsqueeze(2).to_broadcast([p, u, p]),
                                  ALU.is_equal).then_inc(s_match, 1)
                vec.tensor_scalar(to_own[0:p, slot, 0:u], src_g, -1.0, own_row[0:p, 0:1], ALU.mult, ALU.add).then_inc(s_own, 1)
                other_windows = point_next() if point_next else None
                vec.wait_ge(s_hif, g + 1)
                vec.wait_ge(s_score, g + 1)
                for k in range(u):
                    ins = vec.scalar_tensor_tensor(picked[0:p, k, :], iota_row[0:p, 0:BLOCKS], hi_f[0:p, k:k + 1], scores(p, k),
                                                   ALU.is_equal, ALU.mult, accum_out=s_src[0:p, k:k + 1])
                ins.then_inc(s_ssrc, 1)

                def tiles(t, b, banks, n):
                    return t[0:p, b * PER:b * PER + banks * n].rearrange("p (b k) -> p b k", k=n)

                def given_tiles(b, banks, n):
                    return ps[0:p, b:b + banks, 0:n * ROW].rearrange("p b (k c) -> p b k c", c=ROW)

                vec.wait_ge(s_ssrc, g + 1)
                for span in spans(u):
                    ins = vec.tensor_tensor(tiles(z, *span), tiles(s_src, *span), given_tiles(*span)[:, :, :, SCORE], ALU.add)
                ins.then_inc(s_z, 1)
                vec.wait_ge(s_z, g + 1)
                vec.scalar_tensor_tensor(zl[0:p, 0:u], z[0:p, 0:u], ALPHA, z[0:p, 0:u], ALU.mult, ALU.max).then_inc(s_zl, 1)
                vec.wait_ge(s_ez, g + 1)
                vec.tensor_tensor(e[0:p, 0:u], ez[0:p, 0:u], wgt[0:p, slot, 0:u], ALU.mult).then_inc(s_e, 1)
                vec.wait_ge(s_e, g + 1)
                for span in spans(u):
                    b, banks, n = span
                    to = val[0:p, slot, b * PER:b * PER + banks * n, 0:SUM].rearrange("p (b k) c -> p b k c", k=n)
                    ins = vec.tensor_tensor(to, given_tiles(*span)[:, :, :, 0:SUM],
                                            tiles(e, *span).unsqueeze(3).to_broadcast([p, banks, n, SUM]), ALU.mult)
                ins.then_inc(s_val[slot], 1)
                if other_windows:
                    other_windows()

            def place(i, slot, p, u):
                g = 2 * i + slot
                vec.wait_ge(s_sent[slot], BANKS * (i + 1))
                vec.tensor_scalar(before[0:p, 0, 0:u], sent[0:p, slot, 0:u, SUM], bounds[0:p, 0:1], None, ALU.is_ge).then_inc(s_before, 1)
                vec.wait_ge(s_before, g + 1)
                vec.scalar_tensor_tensor(before[0:p, 1, 0:u], sent[0:p, slot, 0:u, SUM + 1], bounds[0:p, 1:2], before[0:p, 0, 0:u],
                                         ALU.is_ge, ALU.max).then_inc(s_later, 1)
                vec.wait_ge(s_later, g + 1)
                vec.wait_ge(s_own, g + 1)
                vec.tensor_tensor(moved[0:p, 0:u], before[0:p, 1, 0:u], to_own[0:p, slot, 0:u], ALU.mult).then_inc(s_moved, 1)
                vec.wait_ge(s_moved, g + 1)
                if not (isinstance(i, int) and i == 0):
                    for j in range(TABLES):
                        vec.wait_ge(s_added[j], adds(i - 1, slot, U, j))
                vec.tensor_tensor(sum_idx[0:p, slot, 0:u], moved[0:p, 0:u], src_f[0:p, slot, 0:u], ALU.add).then_inc(s_idx, 1)

            def turn_of(i, at):
                attend(i, 1, P, U, lambda: point(i + 1, 0, P, U, at(2)))
                place(i, 0, P, U)
                attend(i + 1, 0, P, U, lambda: point(i + 1, 1, P, U, at(3)))
                place(i, 1, P, U)

            point(0, 0, P, U, slice(0, 1))()
            attend(0, 0, P, U, lambda: point(0, 1, P, U, slice(1, 2)))
            turn_of(0, lambda n: slice(n, n + 1))
            with vec.Fori(1, PAIRS - 1) as i:
                turn_of(i, lambda n: bass.ds(2 * i + n, 1))
            attend(PAIRS - 1, 1, P, U, lambda: point(PAIRS, 0, TAIL, 1, slice(GROUPS, GROUPS + 1)))
            place(PAIRS - 1, 0, P, U)
            attend(PAIRS, 0, TAIL, 1)
            place(PAIRS - 1, 1, P, U)
            place(PAIRS, 0, TAIL, 1)

            def add_table(half, t):
                begin, end = HALVES[half]
                n = half * (TABLES - 1) + t - 1
                vec.wait_ge(s_table, 16 * (half + 1))
                vec.wait_ge(s_staged[n % 2], 16 * (n // 2 + 1))
                vec.wait_ge(s_tabled, n)
                vec.tensor_tensor(sums_of(begin, end), sums_of(begin, end), stage_of(n, end - begin), ALU.add).then_inc(s_tabled, 1)

            def spread(t, begin, end):
                return t[:, begin:end].unsqueeze(2).to_broadcast([P, end - begin, D])

            def shares(half):
                begin, end = HALVES[half]
                total = sums_of(begin, end)[:, :, ONE]
                vec.wait_ge(s_tabled, (half + 1) * (TABLES - 1))
                link(vec.tensor_scalar(stat[:, 0, begin:end], total, 0.0, None, ALU.is_equal))
                vec.tensor_scalar(stat[:, 2, begin:end], stat[:, 0, begin:end], -1.0, 1.0, ALU.mult, ALU.add)
                link(vec.tensor_tensor(stat[:, 1, begin:end], total, stat[:, 0, begin:end], ALU.add))
                link(vec.reciprocal(stat[:, 3, begin:end], stat[:, 1, begin:end]))
                link(vec.tensor_tensor(stat[:, 2, begin:end], stat[:, 2, begin:end], stat[:, 3, begin:end], ALU.mult))

            def divide(half):
                begin, end = HALVES[half]
                rows = sums_of(begin, end)[:, :, 0:D]
                link(vec.tensor_tensor(rows, rows, spread(stat[:, 2, :], begin, end), ALU.mult))

            def own_rows(half):
                begin, end = HALVES[half]
                rows = sums_of(begin, end)
                for b in range(begin, end):
                    ins = vec.scalar_tensor_tensor(rows[:, b - begin, 0:D], att[:, b, 0:D], stat[:, 0, b:b + 1], rows[:, b - begin, 0:D],
                                                   ALU.mult, ALU.add)
                ins.then_inc(s_elu, 1)
                vec.wait_ge(s_elu, half + 1)

            def add_positive(half):
                begin, end = HALVES[half]
                link(vec.scalar_tensor_tensor(nodes[:, begin:end, :], sums_of(begin, end)[:, :, 0:D], 0.0, nodes[:, begin:end, :],
                                              ALU.max, ALU.add))

            def add_negative(half):
                begin, end = HALVES[half]
                vec.wait_ge(s_expm, half + 1)
                link(vec.tensor_scalar(att[:, begin:end, 0:D], att[:, begin:end, 0:D], 1.0, -1.0, ALU.min, ALU.add))
                link(vec.tensor_tensor(nodes[:, begin:end, :], nodes[:, begin:end, :], att[:, begin:end, 0:D], ALU.add))

            def scale(half):
                begin, end = HALVES[half]
                vec.wait_ge(s_std, half + 2)
                link(vec.reciprocal(stat[:, 5, begin:end], stat[:, 4, begin:end]))
                vec.scalar_tensor_tensor(stat[:, 6, begin:end], ln_mv[:, begin:end, 0], -1.0, stat[:, 5, begin:end], ALU.mult,
                                         ALU.mult).then_inc(s_scaled, 1)

            for t in range(1, TABLES):
                add_table(0, t)
            shares(0)
            add_table(1, 1)
            divide(0)
            add_table(1, 2)
            own_rows(0)
            add_table(1, 3)
            add_positive(0)
            add_table(1, 4)
            add_negative(0)
            add_table(1, 5)
            moments(*HALVES[0])
            shares(1)
            scale(0)
            divide(1)
            own_rows(1)
            add_positive(1)
            add_negative(1)
            moments(*HALVES[1])
            begin, end = HALVES[1]
            vec.wait_ge(s_std, 3)
            link(vec.reciprocal(stat[:, 5, begin:end], stat[:, 4, begin:end]))
            vec.wait_ge(s_normed[1], SPLIT_AT // BY_CHUNK)
            for c in range(SPLIT_AT // BY_CHUNK, CHUNKS):
                last = min((c + 1) * BY_CHUNK, BLOCKS)
                for b in range(c * BY_CHUNK, last):
                    ins = vec.tensor_scalar(flat[:, b * D:(b + 1) * D], nodes[:, b, :], ln_mv[:, b, 0:1], stat[:, 5, b:b + 1],
                                            ALU.subtract, ALU.mult)
                link(ins)
                rows = flat[:, c * CHUNK:last * D]
                vec.tensor_scalar(rows, rows, 0.0, None, ALU.max).then_inc(s_normed[1], 1)

            vec.wait_ge(s_small, 128)
            for n in range(LAYERS):
                if n == 0:
                    vec.wait_ge(s_copied["gin_in"], CHUNKS)
                else:
                    vec.wait_ge(s_act, chunks_before(n, 0))
                vec.sem_inc(s_agg[n], 1)

                def windows_at(at):
                    return (listed(base_i, at, NODES - 1), listed(first_i, at, GROUPS * MAX_WINDOWS), listed(count_i, at, MAX_WINDOWS))

                def add_attributes(i, slot, p, u, at, own, gathers, windows=None):
                    base, first, count = windows or windows_at(at)
                    rel = dst_rel[0:p, at, 0:u].rearrange("p a k -> p (a k)")
                    vec.wait_ge(s_g[n][slot], 16 * gathers)
                    vec.wait_ge(s_attr[n][slot], 16 * (i + 1))
                    vec.tensor_tensor(gath[0:p, slot, 0:own, 0:D], gath[0:p, slot, 0:own, 0:D], attr[0:p, slot, 0:own, :],
                                      ALU.add).then_inc(s_raw[n][slot], 1)

                    def window_hot(w):
                        vec.scalar_tensor_tensor(
                            hot[0:p, 0:u, :], rel.unsqueeze(2).to_broadcast([p, u, WINDOW]), shifts[0:p, bass.ds(w, 1)],
                            iota_row[0:p, 0:WINDOW].unsqueeze(1).to_broadcast([p, u, WINDOW]),
                            ALU.subtract, ALU.is_equal).then_inc(s_hot[n], 1)

                    def add_window(w):
                        vec.wait_ge(s_win[n], first + w)
                        vec.wait_ge(s_agg[n], first + w)
                        part = agg[:, bass.ds(window_at(base, w), WINDOW)]
                        vec.tensor_tensor(part, part, ps[:, 0, 0:WINDOW], ALU.add).then_inc(s_agg[n], 1)

                    def add_sums():
                        add_window(0)
                        with vec.If(count > 1):
                            with vec.Fori(1, count) as w:
                                window_hot(w)
                                add_window(w)
                        if u == U:
                            vec.sem_inc(s_free[n][slot], 1)
                        else:
                            vec.wait_ge(s_agg[n], first + count)
                            vec.sem_inc(s_summed, 1)

                    window_hot(0)
                    return add_sums

                def spread_sources(q):
                    for t, j in enumerate(PICKED):
                        ins = vec.tensor_scalar(spread_src[:, t, :], ident[:, :], pick_f[:, column(group_of(q, j))], None, ALU.mult)
                    ins.then_inc(s_diag, 1)

                def relate_sources(q, first=False):
                    if not first:
                        vec.wait_ge(s_nodehot[1], pick_no(n, q, 0))
                    vec.wait_ge(s_spread, round_no(n, q))
                    vec.tensor_scalar(src_rel[:, :, :].rearrange("p t e -> p (t e)"), ps[:, 4, 0:len(PICKED) * P], iota_p[:, 0:1], None,
                                      ALU.subtract).then_inc(s_rel, 1)

                def point_nodes(q, j, half):
                    vec.wait_ge(s_pick[half], pick_no(n, q, j) - 1 + NO_PICKS)
                    vec.wait_ge(s_rel, round_no(n, q))
                    for b in range(*HALVES[half]):
                        ins = vec.tensor_scalar(block_in(node_hot, b), src_rel[:, PICKED.index(j), :], float(b * P), None, ALU.is_equal)
                    ins.then_inc(s_nodehot[half], 1)

                def of_round(q, j, windows):
                    return add_attributes(pair_of(q, j), j % 2, P, U, column(group_of(q, j)), tiles_gathered(j), gathered(q, j), windows)

                def rest(t):
                    rows = by_block(flat[:, 0:COLS])
                    vec.wait_ge(s_part, PARTS * n + t + 1)
                    vec.tensor_tensor(rows, rows, first_parts[:, t], ALU.subtract).then_inc(s_rest, 1)

                vec.wait_ge(s_gin_row[n], 16 * CHUNKS)
                rest(0)
                add_sums = add_attributes(0, 0, P, U, slice(0, 1), U, U)
                vec.wait_ge(s_rest, 2 * n + 1)
                rest(1)
                add_sums()
                add_sums = add_attributes(0, 1, P, U, slice(1, 2), U, U)
                spread_sources(0)
                relate_sources(0, first=True)
                point_nodes(0, 1, 0)
                add_sums()

                def round_of(q, last=False):
                    windows = [windows_at(column(group_of(q, 0)))]
                    add_sums = of_round(q, 0, windows[0])
                    point_nodes(q, 1, 1)
                    windows.append(windows_at(column(group_of(q, 1))))
                    add_sums()
                    point_nodes(q, 2, 0)
                    add_sums = of_round(q, 1, windows[1])
                    point_nodes(q, 2, 1)
                    windows.append(windows_at(column(group_of(q, 2))))
                    add_sums()
                    point_nodes(q, 3, 0)
                    add_sums = of_round(q, 2, windows[2])
                    if not last:
                        spread_sources(q + 1)
                    point_nodes(q, 3, 1)
                    windows.append(windows_at(column(group_of(q, 3))))
                    add_sums()
                    if not last:
                        relate_sources(q + 1)
                    add_sums = of_round(q, 3, windows[3])
                    if last:
                        windows.append(windows_at(slice(GROUPS, GROUPS + 1)))
                    else:
                        point_nodes(q + 1, 1, 0)
                    add_sums()
                    return windows[-1]

                with vec.Fori(0, ROUNDS - 1) as q:
                    round_of(q)
                windows = round_of(ROUNDS - 1, last=True)
                add_attributes(PAIRS, 0, TAIL, 1, slice(GROUPS, GROUPS + 1), 1, gathered(ROUNDS, 0) - U + 1, windows)()

                def keep(m, c):
                    to, w = (flat, agg)[m], width(c)
                    vec.wait_ge(s_mm, chunks_before(n, m) + c + 1)
                    vec.tensor_scalar(to[:, c * CHUNK:c * CHUNK + w], ps[:, 4 + c % 4, 0:w], par[:, 3 * m, n:n + 1], None,
                                      ALU.add).then_inc(s_mmv, 1)

                for m in range(2):
                    to = flat if m == 0 else agg
                    if kept_by_dve(m, 0):
                        keep(m, 0)
                    for c in range(CHUNKS):
                        w = width(c)
                        if c + 1 < CHUNKS and kept_by_dve(m, c + 1):
                            keep(m, c + 1)
                        wait_kept(vec, n, m, c)
                        ins = vec.bn_stats(bn[:, c, :], to[:, c * CHUNK:c * CHUNK + w])
                    link(ins)
                    link(vec.bn_aggr(bn_mv[:, :], bn[:, :, :].rearrange("p c s -> p (c s)")))
                    vec.tensor_scalar(bn_t[:, 0:1], bn_mv[:, 1:2], BN_EPS, None, ALU.add).then_inc(s_bnv, 1)
                    vec.wait_ge(s_bns, 2 * n + m + 1)
                    link(vec.reciprocal(bn_t[:, 2:3], bn_t[:, 1:2]))
                    link(vec.tensor_tensor(bn_t[:, 3:4], bn_t[:, 2:3], par[:, 3 * m + 1, n:n + 1], ALU.mult))
                    link(vec.tensor_tensor(bn_t[:, 4:5], bn_mv[:, 0:1], bn_t[:, 3:4], ALU.mult))
                    vec.tensor_tensor(bn_t[:, 5:6], par[:, 3 * m + 2, n:n + 1], bn_t[:, 4:5], ALU.subtract).then_inc(s_bnp, 1)

                name = f"gin_out{n}"
                for c in range(CHUNKS):
                    vec.wait_ge(s_turned[name], c + 1)
                    of = ps[0:LAST, 6 + c % 2, 0:D] if c == CHUNKS - 1 else ps[:, 6 + c % 2, :].rearrange("p (b d) -> p b d", d=D)
                    if n == LAYERS - 1:
                        at = nodes[0:LAST, BLOCKS - 1, :] if c == CHUNKS - 1 else nodes[:, BY_CHUNK * c:BY_CHUNK * (c + 1), :]
                        ins = vec.tensor_tensor(rows_of(flat, c), of, at, ALU.add)
                    else:
                        ins = vec.tensor_copy(rows_of(flat, c), of)
                    ins.then_inc(s_copied[name], 1)

        @block.tensor
        def _(pe):
            def turn(name, of, ready, before=0):
                for c in range(CHUNKS):
                    pe.wait_ge(ready, before + c + 1)
                    if c >= 2:
                        pe.wait_ge(s_copied[name], c - 1)
                    for b, size in blocks_of(c):
                        ins = of(b, size, ps[:, 6 + c % 2, (b % 4) * P:(b % 4 + 1) * P])
                    ins.then_inc(s_turned[name], 1)

            def to_features(b, size, to):
                return pe.transpose(to[:, 0:P], flat[:, b * D:(b + 1) * D], ident[:, :])

            def to_nodes(b, size, to):
                return pe.transpose(to[0:size, :], agg[:, b * P:b * P + size], ident[:, :])

            pe.wait_ge(s_const, 2)
            pe.wait_ge(s_attw, 32)
            pe.transpose(ps[:, 7, 0:D], W_sb[:, 0:D], ident[:, :]).then_inc(s_w_turned, 1)
            pe.wait_ge(s_w_kept, 1)
            pe.matmul(ps[:, 7, 0:2], W_turned, a_sb[:, :], start=True, stop=True).then_inc(s_w_turned, 1)
            pe.wait_ge(s_w_kept, 2)
            turn("att_in", to_features, s_normed[0])
            for b in range(BLOCKS):
                c = b // BY_BANK
                pe.wait_ge(s_copied["att_in"], b // BY_CHUNK + 1)
                if b % BY_BANK == 0 and c >= 2:
                    pe.wait_ge(s_h_kept, c - 1)
                at = b % BY_BANK * ROW
                ins = pe.matmul(ps[:, 4 + c % 2, at:at + ROW], agg[:, b * P:(b + 1) * P], W_sb[:, :], start=True, stop=True)
                if b % BY_BANK == BY_BANK - 1 or b == BLOCKS - 1:
                    ins.then_inc(s_h, 1)

            pe.wait_ge(s_att_ready, 2 * len(PIECES) + 1)
            pe.wait_ge(s_h_kept, FILLS)

            pe.wait_ge(s_windows, 1)

            def listed(t, g, most):
                return pe.value_load(t[0:1, g], min_val=0, max_val=most)

            for slot in range(2):
                pe.sem_inc(s_given[slot], 1)

            def give(i, slot, p, u, at):
                g = 2 * i + slot
                first, count = listed(slot_first_i, at, GROUPS * MAX_WINDOWS), listed(count_i, at, MAX_WINDOWS)
                pe.wait_ge(s_val[1 - slot], i + slot)
                for k in range(u):
                    if k == 0 or score_bank(k - 1) != score_bank(k):
                        pe.matmul(ps[0:p, score_bank(k), CHUNK - 1:CHUNK], zeros[:, 0:p], zeros[:, P:P + 1], start=True, stop=False)
                dst_kj = dst_hot[slot][:, 0:p * u].rearrange("p (j k) -> p k j", k=u)
                with pe.Fori(0, count) as w:
                    pe.wait_ge(s_dsthot[slot], first + w)
                    pe.wait_ge(s_window[slot], 16 * (first + w))
                    for k in range(u):
                        for t in range(PARTS):
                            ins = pe.matmul(given(p, k), dst_kj[:, k, :], window[:, slot, t, :], start=False, stop=False)
                    ins.then_inc(s_given[slot], 1)
                pe.wait_ge(s_lohot, g + 1)
                hot_kj = lo_hot[slot][:, 0:p * u].rearrange("p (j k) -> p k j", k=u)
                for k in range(u):
                    last = k == u - 1 or score_bank(k + 1) != score_bank(k)
                    for t in range(PARTS):
                        ins = pe.matmul(scores(p, k), hot_kj[:, k, :], s1_parts[:, t, :], start=False, stop=last and t == PARTS - 1)
                ins.then_inc(s_score, 1)

            def sum_equal(i, slot, p, u):
                pe.wait_ge(s_val[slot], i + 1)
                pe.wait_ge(s_match, 2 * i + slot + 1)
                pe.wait_ge(s_sent[0], BANKS * (i + slot))
                pe.wait_ge(s_sent[1], BANKS * i)
                for k in range(u):
                    ins = pe.matmul(summed(p, k), match[0:p, slot, k, 0:p], val[0:p, slot, k, :], start=True, stop=True)
                ins.then_inc(s_sums, 1)

            def turn_of(i, at):
                give(i, 1, P, U, at(1))
                sum_equal(i, 0, P, U)
                give(i + 1, 0, P, U, at(2))
                sum_equal(i, 1, P, U)

            give(0, 0, P, U, slice(0, 1))
            turn_of(0, lambda n: slice(n, n + 1))
            with pe.Fori(1, PAIRS - 1) as i:
                turn_of(i, lambda n: bass.ds(2 * i + n, 1))
            give(PAIRS - 1, 1, P, U, slice(GROUPS - 1, GROUPS))
            sum_equal(PAIRS - 1, 0, P, U)
            give(PAIRS, 0, TAIL, 1, slice(GROUPS, GROUPS + 1))
            sum_equal(PAIRS - 1, 1, P, U)
            sum_equal(PAIRS, 0, TAIL, 1)

            turn("gin_in", to_features, s_normed[1])
            pe.wait_ge(s_small, 128)
            for half in range(2):
                pe.sem_inc(s_pick[half], NO_PICKS)

            for n in range(LAYERS):
                def group(i, slot, p, u, first, count, picked):
                    with pe.Fori(0, count) as w:
                        pe.wait_ge(s_msg[n][slot], i + 1)
                        if picked is not None:
                            pe.wait_ge(s_picked, picked + NO_PICKS)
                        pe.wait_ge(s_hot[n], first + w)
                        pe.wait_ge(s_agg[n], first + w)
                        for k in range(u):
                            ins = pe.matmul(ps[:, 0, 0:WINDOW], gath[0:p, slot, k, 0:D], hot[0:p, k, :],
                                            start=(k == 0), stop=(k == u - 1))
                        ins.then_inc(s_win[n], 1)

                def spread_sources(q):
                    pe.wait_ge(s_diag, round_no(n, q))
                    pe.matmul(ps[:, 4, 0:len(PICKED) * P], ones[:, :], spread_src[:, :, :].rearrange("p t e -> p (t e)"),
                              start=True, stop=True).then_inc(s_spread, 1)

                def pick(q, j, half):
                    if half == 0:
                        pe.wait_ge(s_picked, pick_no(n, q, j) - len(PICKED) + NO_PICKS)
                    else:
                        pe.wait_ge(s_attr[n][j % 2], 16 * (pair_of(q, j) + 1))
                    pe.wait_ge(s_nodehot[half], pick_no(n, q, j))
                    for b in range(*HALVES[half]):
                        for t in range(PARTS):
                            ins = pe.matmul(ps[:, j, 0:D], block_in(node_hot, b), part_of(t, b), start=(b == 0 and t == 0), stop=False)
                    if half == 1:
                        ins = pe.matmul(ps[:, j, 0:D], ident[:, :], attr[:, j % 2, U - 1, :], start=False, stop=True)
                    ins.then_inc(s_pick[half], 1)

                def windows_at(at):
                    return listed(first_i, at, GROUPS * MAX_WINDOWS), listed(count_i, at, MAX_WINDOWS)

                def windows_of(i, slot, p, u, at):
                    group(i, slot, p, u, *windows_at(at), None)

                def of_round(q, j, windows):
                    group(pair_of(q, j), j % 2, P, U, *windows, pick_no(n, q, j) if j in PICKED else None)

                windows_of(0, 0, P, U, slice(0, 1))
                spread_sources(0)
                windows_of(0, 1, P, U, slice(1, 2))
                pe.wait_ge(s_part, PARTS * (n + 1))
                pick(0, 1, 0)

                def round_of(q, last=False):
                    of_round(q, 0, windows_at(column(group_of(q, 0))))
                    windows = windows_at(column(group_of(q, 1)))
                    pick(q, 1, 1)
                    pick(q, 2, 0)
                    of_round(q, 1, windows)
                    windows = windows_at(column(group_of(q, 2)))
                    pick(q, 2, 1)
                    pick(q, 3, 0)
                    of_round(q, 2, windows)
                    windows = windows_at(column(group_of(q, 3)))
                    if not last:
                        spread_sources(q + 1)
                    pick(q, 3, 1)
                    tail = windows_at(slice(GROUPS, GROUPS + 1)) if last else None
                    of_round(q, 3, windows)
                    if not last:
                        pick(q + 1, 1, 0)
                    return tail

                with pe.Fori(0, ROUNDS - 1) as q:
                    round_of(q)
                group(PAIRS, 0, TAIL, 1, *round_of(ROUNDS - 1, last=True), None)

                pe.wait_ge(s_summed, n + 1)
                pe.wait_ge(s_gin_row[n], 16 * CHUNKS)
                for m in range(2):
                    of, w_sb = (agg, W1_sb) if m == 0 else (flat, W2_sb)
                    for c in range(CHUNKS):
                        w = width(c)
                        if m == 1:
                            pe.wait_ge(s_act, chunks_before(n, 0) + c + 1)
                        if c >= 4:
                            wait_kept(pe, n, m, c - 4)
                        pe.matmul(ps[:, 4 + c % 4, 0:w], w_sb[:, n, :], of[:, c * CHUNK:c * CHUNK + w],
                                  start=True, stop=True).then_inc(s_mm, 1)
                turn(f"gin_out{n}", to_nodes, s_act, chunks_before(n, 1))


_INS = ["x", "src", "dst", "edge_attr_128", "edge_weight", "L0_gnn_W", "L0_gnn_a", "L1_gnn_W1", "L1_gnn_b1",
        "L1_gnn_g_mlp", "L1_gnn_be_mlp", "L1_gnn_W2", "L1_gnn_b2", "L1_gnn_g_out", "L1_gnn_be_out"]


def kernel(**inputs):
    import numpy as _np
    import concourse.bacc as _bacc
    from concourse import mybir as _mybir
    from concourse.bass_utils import run_bass_kernel_spmd as _run

    nc = _bacc.Bacc("TRN2", target_bir_lowering=False, num_devices=1)
    arrays, args = {}, []
    for name in _INS:
        t = _np.ascontiguousarray(inputs[name])
        arrays[f"in_{name}"] = t
        args.append(nc.dram_tensor(f"in_{name}", t.shape, _mybir.dt.from_np(t.dtype), kind="ExternalInput").ap())
    args.append(nc.dram_tensor("out_nodes", (NODES, D), F32, kind="ExternalOutput").ap())
    build(nc, *args)
    r = _run(nc, [arrays], core_ids=[0])
    return r.results[0]["out_nodes"]
```
